# Optimizing a Trainium2 kernel written in Bass

```python
import numpy as np
import jax
import jax.numpy as jnp

def _softmax(x, axis=-1):
    return jax.nn.softmax(x, axis=axis)

def _gelu(x):
    return jax.nn.gelu(x, approximate=True)

def _silu(x):
    return jax.nn.silu(x)

def _sigmoid(x):
    return jax.nn.sigmoid(x)

def _layernorm(x, axis=-1, eps=1e-05):
    m = jnp.mean(x, axis=axis, keepdims=True)
    v = jnp.var(x, axis=axis, keepdims=True)
    return (x - m) / jnp.sqrt(v + eps)

def _scatter_add(tgt, idx, src, axis=0):
    return tgt.at[idx].add(src)

def _segment_sum(src, seg, n):
    return jax.ops.segment_sum(src, seg, n)
kernel_name = 'mk_seq_postln_d1_jaxref_r8_ce12b5'

def setup_inputs(seed: int=0):
    np.random.seed(seed)
    _w = jnp.asarray

    def _L0_attn_setup():
        import jax, jax.numpy as jnp
        import numpy as np
        LN_EPS = 1e-05
        DENOM_EPS = 1e-06
        NUM_HEADS = 16

        def _layer_norm(x, gamma, beta):
            mu = jnp.mean(x, axis=-1, keepdims=True)
            var = jnp.mean(jnp.square(x - mu), axis=-1, keepdims=True)
            return (x - mu) * jax.lax.rsqrt(var + LN_EPS) * gamma + beta
        key = jax.random.key(seed)
        k1, k2, k3 = jax.random.split(key, 3)
        B, L, D = (4, 512, 128)
        x = jax.random.normal(k1, (B, L, D), dtype=jnp.float32)
        gamma = jnp.ones((D,), dtype=jnp.float32)
        beta = jnp.zeros((D,), dtype=jnp.float32)
        Wqkv = jax.random.normal(k2, (D, 3 * D), dtype=jnp.float32) / np.sqrt(D)
        Wout = jax.random.normal(k3, (D, D), dtype=jnp.float32) / np.sqrt(D)
        return {'x': x, 'gamma': gamma, 'beta': beta, 'Wqkv': Wqkv, 'Wout': Wout}
    _L0_attn_in = _L0_attn_setup()

    def _L0_ffn_setup():
        import jax, jax.numpy as jnp
        import numpy as np
        B, S, D, E, F = (2, 256, 128, 14, 256)
        key = jax.random.key(seed)
        k = jax.random.split(key, 4)
        h = jax.random.normal(k[0], (B, S, D), dtype=jnp.float32)
        router_w = jax.random.normal(k[1], (D, E), dtype=jnp.float32) * 0.02
        w1 = jax.random.uniform(k[2], (E, D, F), dtype=jnp.float32, minval=-1.0, maxval=1.0) * float(np.sqrt(6.0 / D))
        w2 = jax.random.uniform(k[3], (E, F, D), dtype=jnp.float32, minval=-1.0, maxval=1.0) * float(np.sqrt(6.0 / F))
        b1 = jnp.zeros((E, F), dtype=jnp.float32)
        b2 = jnp.zeros((E, D), dtype=jnp.float32)
        return {'h': h, 'router_w': router_w, 'w1': w1, 'b1': b1, 'w2': w2, 'b2': b2}
    _L0_ffn_in = _L0_ffn_setup()
    _d = {'L0_attn_x': _L0_attn_in['x'], 'L0_attn_gamma': _L0_attn_in['gamma'], 'L0_attn_beta': _L0_attn_in['beta'], 'L0_attn_Wqkv': _L0_attn_in['Wqkv'], 'L0_attn_Wout': _L0_attn_in['Wout'], 'L0_ffn_router_w': _L0_ffn_in['router_w'], 'L0_ffn_w1': _L0_ffn_in['w1'], 'L0_ffn_b1': _L0_ffn_in['b1'], 'L0_ffn_w2': _L0_ffn_in['w2'], 'L0_ffn_b2': _L0_ffn_in['b2']}
    _x0 = _d['L0_attn_x']
    _d['L0_attn_x'] = jax.random.normal(jax.random.fold_in(jax.random.key(seed), 1), (2, 1024, 128), dtype=_x0.dtype)
    del _x0
    return _d

def reference(L0_attn_x, L0_attn_gamma, L0_attn_beta, L0_attn_Wqkv, L0_attn_Wout, L0_ffn_router_w, L0_ffn_w1, L0_ffn_b1, L0_ffn_w2, L0_ffn_b2):

    def _L0_attn_ref(x, gamma, beta, Wqkv, Wout):
        import jax, jax.numpy as jnp
        import numpy as np
        LN_EPS = 1e-05
        DENOM_EPS = 1e-06
        NUM_HEADS = 16

        def _layer_norm(x, gamma, beta):
            mu = jnp.mean(x, axis=-1, keepdims=True)
            var = jnp.mean(jnp.square(x - mu), axis=-1, keepdims=True)
            return (x - mu) * jax.lax.rsqrt(var + LN_EPS) * gamma + beta
        B, L, D = x.shape
        H = NUM_HEADS
        HD = D // H
        residual = x
        xn = _layer_norm(x, gamma, beta)
        qkv = (xn @ Wqkv).reshape(B, L, 3, H, HD)
        qkv = jnp.transpose(qkv, (2, 0, 3, 1, 4))
        q, k, v = (qkv[0], qkv[1], qkv[2])
        q = jax.nn.elu(q) + 1.0
        k = jax.nn.elu(k) + 1.0
        kv = jnp.einsum('bhld,bhle->bhde', k, v)
        qkv_out = jnp.einsum('bhld,bhde->bhle', q, kv)
        denom = jnp.einsum('bhld,bhd->bhl', q, k.sum(axis=2)) + DENOM_EPS
        out = qkv_out / denom[..., None]
        out = jnp.transpose(out, (0, 2, 1, 3)).reshape(B, L, D)
        return residual + out @ Wout

    def _L0_ffn_ref(h, router_w, w1, b1, w2, b2):
        import jax, jax.numpy as jnp
        import numpy as np
        B, S, D, E, F = (2, 256, 128, 14, 256)
        Bb, Ss, Dd = h.shape
        x = h.reshape(-1, Dd)
        logits = x @ router_w
        assignments = jnp.argmax(logits, axis=-1)
        probs = jax.nn.softmax(logits, axis=-1)
        weights = jnp.take_along_axis(probs, assignments[:, None], axis=1)[:, 0]
        hid = jnp.einsum('nd,edf->nef', x, w1) + b1
        hid = jax.nn.gelu(hid, approximate=False)
        all_out = jnp.einsum('nef,efd->ned', hid, w2) + b2
        sel = jnp.take_along_axis(all_out, assignments[:, None, None], axis=1)[:, 0, :]
        moe_out = (sel * weights[:, None]).reshape(Bb, Ss, Dd)
        return moe_out
    x = L0_attn_x
    x = _layernorm(x + _L0_attn_ref(x, L0_attn_gamma, L0_attn_beta, L0_attn_Wqkv, L0_attn_Wout), axis=-1)
    x = _layernorm(x + _L0_ffn_ref(x, L0_ffn_router_w, L0_ffn_w1, L0_ffn_b1, L0_ffn_w2, L0_ffn_b2), axis=-1)
    return x

_drawn_inputs = setup_inputs


def setup_inputs(seed=0):
    import zlib

    import numpy as np

    out = dict(_drawn_inputs(seed))
    spreads = {'L0_attn_gamma': (1.0, 0.6),
     'L0_attn_beta': (0.0, 0.1),
     'L0_ffn_b1': (0.0, 0.784),
     'L0_ffn_b2': (0.0, 0.769)}
    factors = {}
    for name, (base, spread) in spreads.items():
        noise = np.random.default_rng([zlib.crc32(name.encode()), seed]).standard_normal(out[name].shape)
        drawn = base * np.exp(spread * noise) if base else spread * noise
        out[name] = jnp.asarray(drawn.astype(out[name].dtype))
    for name, factor in factors.items():
        out[name] = (out[name] * factor).astype(out[name].dtype)
    return out
```

```python
from contextlib import ExitStack

import concourse.bass as bass
from concourse import mybir

F32 = mybir.dt.float32
BF16 = mybir.dt.bfloat16
I32 = mybir.dt.int32
ALU = mybir.AluOpType
ACT = mybir.ActivationFunctionType
AX = mybir.AxisListType.X

P = 128
D = 128
H, HD = 16, 8
E, F = 14, 256
B, S = 2, 1024
NT = B * S // P
C = 4
NC = NT // C
CB = NC // B
JB = S // P
FC = F // P
MAXP = (B * S - E) // P + E
NPG = 30
ROW = D + 2
WB = F + FC
LN_EPS = 1e-5
DENOM_EPS = 1e-6
NOWHERE = 4096
MAGIC = 0x5F3759DF
U = 4
assert MAXP == 29 and (NPG - 2) % U == 0


def build(nc, x, gamma, beta, wqkv, wout, router_w, w1, b1, w2, b2, out):
    with ExitStack() as ctx:
        def sb(name, shape, dt=F32):
            return ctx.enter_context(nc.sbuf_tensor(name, shape, dt))

        def ps(name, shape):
            return ctx.enter_context(nc.psum_tensor(name, shape, F32))

        def sem(name):
            return ctx.enter_context(nc.semaphore(name))

        pages = nc.dram_tensor("pages", [NPG * P, ROW], F32, kind="Internal").ap()
        out_rows = out.rearrange("b s d -> (b s) d")

        ident = sb("ident", [P, P])
        before = sb("before", [P, P], BF16)
        ones = sb("ones", [P, P], BF16)
        head_mask = sb("head_mask", [P, H])
        prio_i = sb("prio_i", [P, E], I32)
        prio = sb("prio", [P, E])
        eidx_i = sb("eidx_i", [P, E], I32)
        eidx = sb("eidx", [P, E])
        pidx_i = sb("pidx_i", [P, 1], I32)
        pidx = sb("pidx", [P, 1])
        empty_row = sb("empty_row", [P, ROW])
        wqkv_sb = sb("wqkv_sb", [P, 3 * D])
        wout_sb = sb("wout_sb", [P, D])
        rw_sb = sb("rw_sb", [P, E])
        vec_rows = sb("vec_rows", [E * FC + 2, P])
        vec_cols = sb("vec_cols", [P, E * FC + 2])
        w1_sb = sb("w1_sb", [P, E, WB])
        w2_sb = sb("w2_sb", [P, E, FC, D])
        b2_rows = sb("b2_rows", [E, D])
        b2_rest = sb("b2_rest", [E, 2, D])
        b2_part = sb("b2_part", [E, 3, D], BF16)
        b2_k = sb("b2_k", [P, E * D], BF16)

        x_sb = sb("x_sb", [P, NT, D])
        stats = sb("stats", [P, NT, 6])
        mv = sb("mv", [P, NT, 2])
        stats2 = sb("stats2", [P, NT, 6])
        mv2 = sb("mv2", [P, NT, 2])
        rstd = sb("rstd", [P, NT])
        shift = sb("shift", [P, NT])
        rstd2 = sb("rstd2", [P, NT])
        shift2 = sb("shift2", [P, NT])
        nt_ve = sb("nt_ve", [P, C])
        nt_half = sb("nt_half", [P, C], I32)
        nt_y = sb("nt_y", [P, 4, C])
        nt_a = sb("nt_a", [P, 3, C])
        nt_b = sb("nt_b", [P, 3, C])
        xn = sb("xn", [P, NT, D])
        xn_t = sb("xn_t", [P, NT, P])
        q_exp = sb("q_exp", [P, NT * P])
        q_pos = sb("q_pos", [P, NT * P])
        q_t = sb("q_t", [P, NT, P])
        k_exp = sb("k_exp", [P, NT, D])
        k_pos = sb("k_pos", [P, NT, D])
        k_sb = sb("k_sb", [P, NT, D])
        v_sb = sb("v_sb", [P, NT, D + 1])
        kv_h = sb("kv_h", [P, B, D + H])
        den = sb("den", [P, C, H])
        rden = sb("rden", [P, C, H])
        att = sb("att", [P, NT, D])
        att_t = sb("att_t", [P, NT, P])
        pre = sb("pre", [P, NT, D])
        rows = sb("rows", [P, NT, ROW])
        x1_t = sb("x1_t", [P, NT, P])

        top = sb("top", [P, NT])
        is_top = sb("is_top", [P, C, E])
        ranked = sb("ranked", [P, C, E])
        first = sb("first", [P, NT])
        chosen = sb("chosen", [P, NC, C + 1, E], BF16)
        below = sb("below", [P, NT, E])
        e_exp = sb("e_exp", [P, NT, E])
        e_sum = sb("e_sum", [P, NT])
        cnt = sb("cnt", [P, NC + 1, E])
        cap = sb("cap", [P, NC + 1, E])
        base = sb("base", [P, NC + 1, E])
        used = sb("used", [P, NC + 1])
        cnt_i = sb("cnt_i", [P, E], I32)
        pg_i = sb("pg_i", [P, E], I32)
        LEAD = 8
        pref = sb("pref", [P, 5, LEAD + E])
        start_pg = sb("start_pg", [P, E])
        end_pg = sb("end_pg", [P, E])
        jump = sb("jump", [P, E])
        gets = sb("gets", [P, E])
        room = sb("room", [P, E])
        low = sb("low", [P, E])
        over = sb("over", [P, C, E])
        slot_a = sb("slot_a", [P, C, E])
        slot_b = sb("slot_b", [P, C, E])
        slot_c = sb("slot_c", [P, C, E])
        slot = sb("slot", [P, NT], I32)
        own_a = sb("own_a", [P, E])
        own_b = sb("own_b", [P, E])
        own_c = sb("own_c", [P, E])
        own = sb("own", [P, NC + 1])
        own_sum = sb("own_sum", [P, 1])
        page_e = sb("page_e", [1, 32], I32)

        xs = sb("xs", [P, U, D])
        xr = sb("xr", [P, NPG, ROW])
        xs_t = sb("xs_t", [P, U, P])
        w1_cur = sb("w1_cur", [P, U, WB])
        hid = sb("hid", [P, U, FC, P])
        res = sb("res", [P, U, D])
        st3 = sb("st3", [P, U, 6])
        agg = sb("agg", [P, 5, U])
        mv3 = sb("mv3", [P, 2, U])
        rstd3 = sb("rstd3", [P, U])
        shift3 = sb("shift3", [P, U])
        token = sb("token", [P, U], I32)
        y_out = sb("y_out", [P, U, D])

        ps_t = ps("ps_t", [P, C, P])
        ps_q = ps("ps_q", [P, C * P])
        ps_kv = ps("ps_kv", [P, C, 2 * D])
        ps_acc = ps("ps_acc", [P, 512])
        ps_num = ps("ps_num", [P, 2, 512])
        ps_o = ps("ps_o", [P, C, P])
        ps_kvh = ps_acc[:, 0:D + 1]
        ps_vec = ps_acc[:, 0:E * FC + 2]
        num_v = ps_num[:, :, 0:2 * (D + H)].rearrange("p b (i n) -> p b i n", i=2)

        def ps_lg(c):
            bank = ps_kv[:, 0, :] if c % 2 else ps_q
            return bank[:, 0:C * E].rearrange("p (i e) -> p i e", e=E)

        def ps_rk(c):
            bank = ps_kv[:, 2, :] if c % 2 else ps_acc
            return bank[:, 0:(C + 1) * E].rearrange("p (i e) -> p i e", e=E)

        ps_row = ps_acc[0:1, 0:32]
        ps_xt = [ps_t[:, 0, :], ps_q[:, 0:P]]
        ps_h = [ps_kv[:, 0, :].rearrange("p (c n) -> p c n", c=FC), ps_kv[:, 2, :].rearrange("p (c n) -> p c n", c=FC)]
        ps_y = [ps_num[:, 0, 0:D], ps_num[:, 1, 0:D]]

        x_in = [sem(f"x_in{c}") for c in range(NC)]
        vec_in, wqkv_in, wout_in, rw_in = sem("vec_in"), sem("wqkv_in"), sem("wout_in"), sem("rw_in")
        w1_in, w2_in, b2_in, b2k_in = sem("w1_in"), sem("w2_in"), sem("b2_in"), sem("b2k_in")
        pages_clear = sem("pages_clear")
        pool_c = sem("pool_c")
        v_ones = sem("v_ones")
        vec_ps, vec_ok, b1_ok = sem("vec_ps"), sem("vec_ok"), sem("b1_ok")
        consts_ok = sem("consts_ok")
        b2_split, b2k_zero = sem("b2_split"), sem("b2k_zero")
        dve_s = sem("dve_s")
        stat_ok = sem("stat_ok")
        xn_ok = sem("xn_ok")
        xt_ps, xt_ok = sem("xt_ps"), sem("xt_ok")
        q_ps, kv_ps = sem("q_ps"), sem("kv_ps")
        q_act, k_act, v_ok = sem("q_act"), sem("k_act"), sem("v_ok")
        q_ok, k_ok = sem("q_ok"), sem("k_ok")
        kvh_ps, kvh_ok = sem("kvh_ps"), sem("kvh_ok")
        num_ps, att_ok = sem("num_ps"), sem("att_ok")
        at_ps, at_ok = sem("at_ps"), sem("at_ok")
        wo_ps, pre_ok = sem("wo_ps"), sem("pre_ok")
        x1_ok, x1t_ps, x1t_ok = sem("x1_ok"), sem("x1t_ps"), sem("x1t_ok")
        lg_ps, chosen_ok, below_ok, eexp_ok = sem("lg_ps"), sem("chosen_ok"), sem("below_ok"), sem("eexp_ok")
        weight_ok = sem("weight_ok")
        rk_ps, slot_ok = sem("rk_ps"), sem("slot_ok")
        rows_out = sem("rows_out")
        own_ok, row_ps, page_e_ok = sem("own_ok"), sem("row_ps"), sem("page_e_ok")
        xs_in = [sem(f"xs_in{i}") for i in range(2)]
        xr_in = [sem(f"xr_in{i}") for i in range(2)]
        px_ps, px_ok = sem("px_ps"), sem("px_ok")
        w1_ok, h_ps, hid_ok, y_ps, res_ok = sem("w1_ok"), sem("h_ps"), sem("hid_ok"), sem("y_ps"), sem("res_ok")
        y_ok, token_ok = sem("y_ok"), sem("token_ok")
        out_in = [sem(f"out_in{k}") for k in range(U)]

        block = ctx.enter_context(nc.Block())

        N_CONSTS = 9
        (P_IDENT0, P_IDENT, P_BEF0, P_BEFORE, P_ONES, P_HM0, P_HM1, P_HEAD, P_PRIO, P_EIDX, P_PIDX, P_EMPTY0,
         P_EMPTY, P_TOKENS) = range(1, 15)

        @block.sync
        def _(sp):
            def load_x(c):
                b, h = c // CB, c % CB
                src = x[b].rearrange("(p j) d -> p j d", j=JB)[:, C * h:C * h + C, :]
                sp.dma_start(x_sb[:, C * c:C * c + C, :], src).then_inc(x_in[c], 16)

            load_x(0)
            load_x(1)
            load_x(2)
            load_x(3)
            sp.dma_start(wout_sb[:], wout).then_inc(wout_in, 16)
            sp.dma_start(rw_sb[:], router_w).then_inc(rw_in, 16)
            sp.wait_ge(pool_c, P_EMPTY)
            sp.dma_start(pages.rearrange("(j p) d -> p j d", p=P),
                         empty_row[:].unsqueeze(1).to_broadcast([P, NPG, ROW])).then_inc(pages_clear, 16)
            sp.dma_start(w1_sb[:, :, 0:F], w1.rearrange("e d f -> d e f")).then_inc(w1_in, 16)
            sp.dma_start(w2_sb[:], w2.rearrange("e (c f) d -> f e c d", f=P)).then_inc(w2_in, 16)
            sp.wait_ge(b2_split, 1)
            sp.wait_ge(b2k_zero, 1)
            for i in range(3):
                sp.dma_start(b2_k[i:i + 1, :], b2_part[:, i, :]).then_inc(b2k_in, 16)

            def load_pair(q, half, ring_free=None, seen=None):
                if ring_free is not None:
                    sp.wait_ge(px_ps, ring_free)
                    sp.wait_ge(xr_in[half], seen)
                src = pages[bass.ds(q * (2 * P), 2 * P), :].rearrange("(j p) d -> p j d", p=P)
                sp.dma_start(xs[:, 2 * half:2 * half + 2, :], src[:, :, 0:D]).then_inc(xs_in[half], 16)
                sp.dma_start(xr[:, bass.ds(q * 2, 2), :], src).then_inc(xr_in[half], 16)

            sp.wait_ge(rows_out, 16 * NT)
            load_pair(0, 0)
            load_pair(1, 1)
            with sp.Fori(0, (NPG - 4) // U) as i:
                load_pair(2 * i + 2, 0, ring_free=4 * i + 2, seen=16 * i + 16)
                load_pair(2 * i + 3, 1, ring_free=4 * i + 4, seen=16 * i + 16)
            load_pair(NPG // 2 - 1, 0, ring_free=NPG - 4, seen=16 * (NPG // 4))
            for k in range(U):
                sp.wait_ge(out_in[k], 16 * ((MAXP - 1) // U + (1 if k == 0 else 0)))

        @block.gpsimd
        def _(pool):
            pool.memset(ident[:], 0.0).then_inc(pool_c, 1)
            pool.wait_ge(pool_c, P_IDENT0)
            pool.affine_select(out=ident[:], in_=ident[:], compare_op=ALU.not_equal, fill=1.0, base=0,
                               pattern=[[-1, P]], channel_multiplier=1).then_inc(pool_c, 1)
            pool.memset(before[:], 1.0).then_inc(pool_c, 1)
            pool.wait_ge(pool_c, P_BEF0)
            pool.affine_select(out=before[:], in_=before[:], compare_op=ALU.is_gt, fill=0.0, base=0,
                               pattern=[[1, P]], channel_multiplier=-1).then_inc(pool_c, 1)
            pool.memset(ones[:], 1.0).then_inc(pool_c, 1)
            pool.memset(head_mask[:], 1.0).then_inc(pool_c, 1)
            pool.wait_ge(pool_c, P_HM0)
            pool.affine_select(out=head_mask[:], in_=head_mask[:], compare_op=ALU.is_ge, fill=0.0, base=0,
                               pattern=[[-HD, H]], channel_multiplier=1).then_inc(pool_c, 1)
            pool.wait_ge(pool_c, P_HM1)
            pool.affine_select(out=head_mask[:], in_=head_mask[:], compare_op=ALU.is_ge, fill=0.0, base=HD - 1,
                               pattern=[[HD, H]], channel_multiplier=-1).then_inc(pool_c, 1)
            pool.iota(prio_i[:], pattern=[[-1, E]], base=E, channel_multiplier=0).then_inc(pool_c, 1)
            pool.iota(eidx_i[:], pattern=[[1, E]], base=0, channel_multiplier=0).then_inc(pool_c, 1)
            pool.iota(pidx_i[:], pattern=[[1, 1]], base=0, channel_multiplier=1).then_inc(pool_c, 1)
            pool.memset(empty_row[:, 0:D + 1], 0.0).then_inc(pool_c, 1)
            pool.iota(empty_row[:, D + 1:ROW].bitcast(I32), pattern=[[1, 1]], base=NOWHERE,
                      channel_multiplier=1).then_inc(pool_c, 1)
            for b in range(B):
                t = pool.iota(rows[:, b * JB:(b + 1) * JB, D + 1].bitcast(I32), pattern=[[1, JB]], base=b * S,
                              channel_multiplier=JB)
            t.then_inc(pool_c, 1)
            pool.memset(v_sb[:, :, D:D + 1], 1.0).then_inc(v_ones, 1)

            for c in range(1, NC):
                pool.wait_ge(x_in[c], 16)
                pool.wait_ge(stat_ok, c + 1)
                for t in range(C * c, C * c + C):
                    pool.tensor_scalar(xn[:, t, :], x_sb[:, t, :], rstd[:, t:t + 1], shift[:, t:t + 1],
                                       ALU.mult, ALU.add).then_inc(xn_ok, 1)

            last_slot = pool.to_reg(NPG * P - 1)
            pool.wait_ge(pages_clear, 16)
            pool.wait_ge(pool_c, P_TOKENS)
            for c in range(NC):
                pool.wait_ge(x1_ok, c + 1)
                pool.wait_ge(weight_ok, c + 1)
                pool.wait_ge(slot_ok, c + 1)
                for t in range(C * c, C * c + C):
                    pool.indirect_dma_start(pages, bass.IndirectOffsetOnAxis(ap=slot[:, t:t + 1], axis=0),
                                            rows[:, t, :], None, bounds_check=last_slot,
                                            oob_is_err=False).then_inc(rows_out, 16)

            last_token = pool.to_reg(B * S - 1)

            wanted = pool.alloc_register("wanted")
            pool.reg_mov(wanted, 0)

            def store(k):
                pool.reg_add(wanted, wanted, 2)
                pool.wait_ge(page_e_ok, 1)
                pool.wait_ge(y_ok, wanted)
                pool.indirect_dma_start(out_rows, bass.IndirectOffsetOnAxis(ap=token[:, k:k + 1], axis=0),
                                        y_out[:, k, :], None, bounds_check=last_token,
                                        oob_is_err=False).then_inc(out_in[k], 16)

            with pool.Fori(0, MAXP // U):
                for k in range(U):
                    store(k)
            store(0)

        @block.scalar
        def _(act):
            act.dma_start(vec_rows[0:E * FC, :], b1.rearrange("e (c f) -> (e c) f", c=FC)).then_inc(vec_in, 16)
            act.dma_start(vec_rows[E * FC:E * FC + 1, :], gamma.rearrange("(a d) -> a d", a=1)).then_inc(vec_in, 16)
            act.dma_start(vec_rows[E * FC + 1:E * FC + 2, :], beta.rearrange("(a d) -> a d", a=1)).then_inc(vec_in, 16)
            act.dma_start(wqkv_sb[:], wqkv).then_inc(wqkv_in, 16)
            act.dma_start(b2_rows[:], b2).then_inc(b2_in, 16)

            def xt(c):
                act.wait_ge(xt_ps, c + 1)
                act.activation(xn_t[:, C * c:C * c + C, :], ps_t[:], ACT.Identity, bias=vec_cols[:, E * FC + 1:E * FC + 2],
                               scale=vec_cols[:, E * FC:E * FC + 1]).then_inc(xt_ok, 1)

            def q(c):
                act.wait_ge(q_ps, c + 1)
                act.activation(q_exp[:, c * C * P:(c + 1) * C * P], ps_q[:], ACT.Exp).then_inc(q_act, 1)
                act.activation(q_pos[:, c * C * P:(c + 1) * C * P], ps_q[:], ACT.Relu).then_inc(q_act, 1)

            def kv(c):
                act.wait_ge(kv_ps, c + 1)
                act.activation(k_exp[:, C * c:C * c + C, :], ps_kv[:, :, 0:D], ACT.Exp).then_inc(k_act, 1)
                act.activation(k_pos[:, C * c:C * c + C, :], ps_kv[:, :, 0:D], ACT.Relu).then_inc(k_act, 1)
                act.copy(v_sb[:, C * c:C * c + C, 0:D], ps_kv[:, :, D:2 * D]).then_inc(v_ok, 1)

            def at(c):
                act.wait_ge(at_ps, c + 1)
                act.copy(att_t[:, C * c:C * c + C, :], ps_o[:]).then_inc(at_ok, 1)

            def x1t(c):
                act.wait_ge(x1t_ps, c + 1)
                act.copy(x1_t[:, C * c:C * c + C, :], ps_t[:]).then_inc(x1t_ok, 1)

            def eexp(c):
                act.wait_ge(below_ok, c + 1)
                act.activation(e_exp[:, C * c:C * c + C, :], below[:, C * c:C * c + C, :], ACT.Exp).then_inc(eexp_ok, 1)

            act.wait_ge(vec_ok, 1)
            xt(0)
            q(0)
            xt(1)
            kv(0)
            q(1)
            kv(1)
            xt(2)
            q(2)
            at(0)
            kv(2)
            at(1)
            xt(3)
            q(3)
            x1t(0)
            kv(3)
            x1t(1)
            eexp(0)
            at(2)
            eexp(1)
            at(3)
            x1t(2)
            x1t(3)
            eexp(2)
            eexp(3)

            def page_t(j, k):
                act.wait_ge(px_ps, j + 1)
                act.copy(xs_t[:, k, :], ps_xt[k % 2]).then_inc(px_ok, 1)

            def gelu(j, k):
                act.wait_ge(h_ps, j + 1)
                for c in range(FC):
                    act.activation(hid[:, k, c, :], ps_h[k % 2][:, c, :], ACT.Gelu,
                                   bias=w1_cur[:, k, F + c:F + c + 1]).then_inc(hid_ok, 1)

            page_t(0, 0)
            page_t(1, 1)
            gelu(0, 0)
            with act.Fori(0, (NPG - 2) // U) as i:
                for k in range(U):
                    page_t(U * i + k + 2, (k + 2) % U)
                    gelu(U * i + k + 1, (k + 1) % U)

        @block.vector
        def _(dve):
            links = [0]

            def link(ins):
                links[0] += 1
                ins.then_inc(dve_s, 1)
                dve.wait_ge(dve_s, links[0])

            def newton(var, mean, n, rstd_o, shift_o, done=None, linked=None):
                ln = linked or link
                y = [nt_y[:, s, 0:n] for s in range(3)] + [rstd_o]
                ln(dve.tensor_scalar(nt_ve[:, 0:n], var, LN_EPS, None, ALU.add))
                ln(dve.tensor_scalar(nt_half[:, 0:n], nt_ve[:, 0:n].bitcast(I32), 1, None, ALU.logical_shift_right))
                ln(dve.tensor_scalar(y[0].bitcast(I32), nt_half[:, 0:n], -1.0, float(MAGIC), ALU.mult, ALU.add))
                for s in range(3):
                    ln(dve.scalar_tensor_tensor(out=nt_a[:, s, 0:n], in0=y[s], scalar=-0.5, in1=y[s],
                                                op0=ALU.mult, op1=ALU.mult))
                    ln(dve.tensor_tensor(nt_b[:, s, 0:n], nt_a[:, s, 0:n], nt_ve[:, 0:n], ALU.mult))
                    ln(dve.scalar_tensor_tensor(out=y[s + 1], in0=nt_b[:, s, 0:n], scalar=1.5, in1=y[s],
                                                op0=ALU.add, op1=ALU.mult))
                last = dve.scalar_tensor_tensor(out=shift_o, in0=mean, scalar=-1.0, in1=rstd_o,
                                                op0=ALU.mult, op1=ALU.mult)
                if done is not None:
                    last.then_inc(done, 1)
                else:
                    ln(last)

            dve.wait_ge(pool_c, P_PIDX)
            dve.tensor_copy(prio[:], prio_i[:]).then_inc(consts_ok, 1)
            dve.tensor_copy(eidx[:], eidx_i[:]).then_inc(consts_ok, 1)
            dve.tensor_copy(pidx[:], pidx_i[:]).then_inc(consts_ok, 1)
            for z in (cnt, cap, base):
                dve.memset(z[:, 0, :], 0.0).then_inc(consts_ok, 1)
            dve.memset(used[:, 0:1], 0.0).then_inc(consts_ok, 1)
            dve.memset(pref[:, :, 0:LEAD], 0.0).then_inc(consts_ok, 1)
            dve.memset(chosen[:, :, C, :], 0.0).then_inc(consts_ok, 1)

            def norm1(c):
                dve.wait_ge(x_in[c], 16)
                ts = range(C * c, C * c + C)
                for t in ts:
                    last = dve.bn_stats(stats[:, t, :], x_sb[:, t, :])
                link(last)
                for t in ts:
                    last = dve.bn_aggr(mv[:, t, :], stats[:, t, :])
                link(last)
                newton(mv[:, C * c:C * c + C, 1], mv[:, C * c:C * c + C, 0], C, rstd[:, C * c:C * c + C],
                       shift[:, C * c:C * c + C], done=stat_ok)

            norm1(0)
            dve.wait_ge(stat_ok, 1)
            for t in range(C):
                dve.tensor_scalar(xn[:, t, :], x_sb[:, t, :], rstd[:, t:t + 1], shift[:, t:t + 1],
                                  ALU.mult, ALU.add).then_inc(xn_ok, 1)
            dve.wait_ge(vec_ps, 1)
            dve.tensor_copy(vec_cols[:], ps_vec).then_inc(vec_ok, 1)
            norm1(1)
            dve.wait_ge(b2_in, 16)
            link(dve.tensor_copy(b2_part[:, 0, :], b2_rows[:]))
            link(dve.tensor_tensor(b2_rest[:, 0, :], b2_rows[:], b2_part[:, 0, :], ALU.subtract))
            link(dve.tensor_copy(b2_part[:, 1, :], b2_rest[:, 0, :]))
            link(dve.tensor_tensor(b2_rest[:, 1, :], b2_rest[:, 0, :], b2_part[:, 1, :], ALU.subtract))
            dve.tensor_copy(b2_part[:, 2, :], b2_rest[:, 1, :]).then_inc(b2_split, 1)
            dve.memset(b2_k[:].bitcast(I32), 0).then_inc(b2k_zero, 1)

            def elu_q(c):
                o = slice(c * C * P, (c + 1) * C * P)
                dve.wait_ge(q_act, 2 * c + 2)
                dve.scalar_tensor_tensor(out=q_t[:, C * c:C * c + C, :].rearrange("p i n -> p (i n)"), in0=q_exp[:, o],
                                         scalar=1.0, in1=q_pos[:, o], op0=ALU.min, op1=ALU.add).then_inc(q_ok, 1)

            def elu_k(c):
                o = slice(C * c, C * c + C)
                dve.wait_ge(k_act, 2 * c + 2)
                dve.scalar_tensor_tensor(out=k_sb[:, o, :], in0=k_exp[:, o, :], scalar=1.0, in1=k_pos[:, o, :],
                                         op0=ALU.min, op1=ALU.add).then_inc(k_ok, 1)

            def heads(b):
                dve.wait_ge(kvh_ps, b + 1)
                dve.wait_ge(pool_c, P_HEAD)
                dve.tensor_tensor(kv_h[:, b, 0:D].rearrange("p (h e) -> p h e", e=HD),
                                  ps_kvh[:, 0:D].rearrange("p (h e) -> p h e", e=HD),
                                  head_mask[:].unsqueeze(2).to_broadcast([P, H, HD]), ALU.mult).then_inc(kvh_ok, 1)
                dve.tensor_scalar(kv_h[:, b, D:D + H], head_mask[:], ps_kvh[:, D:D + 1], None,
                                  ALU.mult).then_inc(kvh_ok, 1)

            def divide(c):
                dve.wait_ge(num_ps, c + 1)
                link(dve.tensor_scalar(den[:].rearrange("p (b i) h -> p b i h", b=2), num_v[:, :, :, D:D + H],
                                       DENOM_EPS, None, ALU.add))
                link(dve.reciprocal(rden[:], den[:]))
                for b in range(2):
                    t = C * c + 2 * b
                    dve.tensor_tensor(att[:, t:t + 2, :].rearrange("p i (h e) -> p i h e", e=HD),
                                      num_v[:, b, :, 0:D].rearrange("p i (h e) -> p i h e", e=HD),
                                      rden[:, 2 * b:2 * b + 2, :].unsqueeze(3).to_broadcast([P, 2, H, HD]),
                                      ALU.mult).then_inc(att_ok, 1)

            def norm2(c):
                ts = range(C * c, C * c + C)
                dve.wait_ge(wo_ps, c + 1)
                dve.scalar_tensor_tensor(out=pre[:, C * c:C * c + C, :], in0=x_sb[:, C * c:C * c + C, :], scalar=2.0,
                                         in1=ps_o[:], op0=ALU.mult, op1=ALU.add).then_inc(pre_ok, 1)
                dve.wait_ge(pre_ok, c + 1)
                for t in ts:
                    last = dve.bn_stats(stats2[:, t, :], pre[:, t, :])
                link(last)
                for t in ts:
                    last = dve.bn_aggr(mv2[:, t, :], stats2[:, t, :])
                link(last)
                newton(mv2[:, C * c:C * c + C, 1], mv2[:, C * c:C * c + C, 0], C, rstd2[:, C * c:C * c + C],
                       shift2[:, C * c:C * c + C])
                for t in ts:
                    last = dve.tensor_scalar(rows[:, t, 0:D], pre[:, t, :], rstd2[:, t:t + 1], shift2[:, t:t + 1],
                                             ALU.mult, ALU.add)
                last.then_inc(x1_ok, 1)

            def route(c):
                o = slice(C * c, C * c + C)
                lg = ps_lg(c)
                prio_b = prio[:].unsqueeze(1).to_broadcast([P, C, E])
                top_b = top[:, o].unsqueeze(2).to_broadcast([P, C, E])
                dve.wait_ge(lg_ps, c + 1)
                link(dve.tensor_reduce(top[:, o], lg, AX, ALU.max))
                link(dve.tensor_tensor(is_top[:], lg, top_b, ALU.is_equal))
                link(dve.tensor_tensor(ranked[:], is_top[:], prio_b, ALU.mult))
                link(dve.tensor_reduce(first[:, o], ranked[:], AX, ALU.max))
                dve.tensor_tensor(chosen[:, c, 0:C, :], prio_b, first[:, o].unsqueeze(2).to_broadcast([P, C, E]),
                                  ALU.is_equal).then_inc(chosen_ok, 1)
                dve.tensor_tensor(below[:, o, :], lg, top_b, ALU.subtract).then_inc(below_ok, 1)

            def weigh(c):
                o = slice(C * c, C * c + C)
                dve.wait_ge(eexp_ok, c + 1)
                link(dve.tensor_reduce(e_sum[:, o], e_exp[:, o, :], AX, ALU.add))
                dve.reciprocal(rows[:, o, D], e_sum[:, o]).then_inc(weight_ok, 1)

            def place(c):
                rk = ps_rk(c)

                def each(a):
                    return a.unsqueeze(1).to_broadcast([P, C, E])

                link(dve.tensor_tensor(room[:], cap[:, c, :], cnt[:, c, :], ALU.subtract))
                link(dve.tensor_tensor(low[:], base[:, c, :], cnt[:, c, :], ALU.add))
                dve.wait_ge(rk_ps, c + 1)
                link(dve.tensor_tensor(cnt[:, c + 1, :], cnt[:, c, :], rk[:, C, :], ALU.add))
                link(dve.tensor_scalar(cnt_i[:], cnt[:, c + 1, :], float(P - 1), None, ALU.add))
                link(dve.tensor_scalar(pg_i[:], cnt_i[:], 7, None, ALU.logical_shift_right))
                link(dve.tensor_scalar(cap[:, c + 1, :], pg_i[:], float(P), None, ALU.mult))
                link(dve.tensor_tensor(gets[:], cap[:, c + 1, :], cap[:, c, :], ALU.subtract))
                link(dve.tensor_scalar(pref[:, 0, LEAD:], gets[:], 1.0 / P, None, ALU.mult))
                for s, d in enumerate((1, 2, 4, 8)):
                    link(dve.tensor_tensor(pref[:, s + 1, LEAD:], pref[:, s, LEAD:], pref[:, s, LEAD - d:LEAD - d + E],
                                           ALU.add))
                total = pref[:, 4, LEAD:]
                link(dve.scalar_tensor_tensor(out=start_pg[:], in0=total, scalar=used[:, c:c + 1],
                                              in1=pref[:, 0, LEAD:], op0=ALU.add, op1=ALU.subtract))
                link(dve.scalar_tensor_tensor(out=jump[:], in0=start_pg[:], scalar=float(P), in1=cap[:, c, :],
                                              op0=ALU.mult, op1=ALU.subtract))
                link(dve.tensor_tensor(jump[:], jump[:], base[:, c, :], ALU.subtract))
                link(dve.tensor_tensor(over[:], rk[:, 0:C, :], each(room[:]), ALU.is_ge))
                link(dve.tensor_tensor(slot_a[:], over[:], each(jump[:]), ALU.mult))
                link(dve.tensor_tensor(slot_b[:], rk[:, 0:C, :], each(low[:]), ALU.add))
                link(dve.tensor_tensor(slot_c[:], slot_a[:], slot_b[:], ALU.add))
                link(dve.tensor_tensor(slot_a[:], slot_c[:], chosen[:, c, 0:C, :], ALU.mult))
                with nc.allow_low_precision(reason="slots are whole numbers below 2**24"):
                    dve.tensor_reduce(slot[:, C * c:C * c + C], slot_a[:], AX, ALU.add).then_inc(slot_ok, 1)
                link(dve.tensor_scalar(used[:, c + 1:c + 2], pref[:, 4, LEAD + E - 1:LEAD + E], used[:, c:c + 1], None,
                                       ALU.add))
                link(dve.tensor_scalar(own_a[:], start_pg[:], pidx[:, 0:1], None, ALU.is_le))
                link(dve.tensor_tensor(end_pg[:], start_pg[:], pref[:, 0, LEAD:], ALU.add))
                link(dve.scalar_tensor_tensor(out=own_b[:], in0=end_pg[:], scalar=pidx[:, 0:1], in1=own_a[:],
                                              op0=ALU.is_gt, op1=ALU.mult))
                link(dve.tensor_tensor(own_c[:], own_b[:], eidx[:], ALU.mult))
                link(dve.tensor_reduce(own[:, c + 1:c + 2], own_c[:], AX, ALU.add))
                link(dve.scalar_tensor_tensor(out=gets[:], in0=gets[:], scalar=0.0, in1=jump[:], op0=ALU.is_gt,
                                              op1=ALU.mult))
                link(dve.tensor_tensor(base[:, c + 1, :], base[:, c, :], gets[:], ALU.add))

            elu_q(0)
            elu_k(0)
            norm1(2)
            elu_q(1)
            elu_k(1)
            dve.wait_ge(consts_ok, N_CONSTS)
            heads(0)
            norm1(3)
            divide(0)
            elu_q(2)
            norm2(0)
            divide(1)
            elu_k(2)
            elu_q(3)
            norm2(1)
            elu_k(3)
            route(0)
            heads(1)
            weigh(0)
            route(1)
            place(0)
            divide(2)
            weigh(1)
            divide(3)
            place(1)
            norm2(2)
            norm2(3)
            route(2)
            place(2)
            route(3)
            place(3)
            dve.tensor_reduce(own_sum[:], own[:, 1:NC + 1], AX, ALU.add).then_inc(own_ok, 1)
            weigh(2)
            weigh(3)
            dve.wait_ge(row_ps, 1)
            dve.tensor_copy(page_e[:], ps_row).then_inc(page_e_ok, 1)
            dve.wait_ge(w1_in, 16)
            link(dve.tensor_copy(w1_sb[:, :, F:WB], vec_cols[:, 0:E * FC].rearrange("p (e c) -> p e c", c=FC)))
            dve.wait_ge(page_e_ok, 1)

            before_loop = links[0]

            def fetch_w1(j, k):
                e = dve.value_load(page_e[0:1, bass.ds(j, 1)], min_val=0, max_val=E - 1)
                dve.tensor_copy(w1_cur[:, k, :], w1_sb[:, bass.ds(e, 1), :].rearrange("p a n -> p (a n)")).then_inc(w1_ok, 1)

            def residual(j, k, n):
                dve.wait_ge(y_ps, j + 1)
                dve.scalar_tensor_tensor(out=res[:, k, :], in0=ps_y[k % 2],
                                         scalar=xr[:, bass.ds(j, 1), D:D + 1].rearrange("p a n -> p (a n)"),
                                         in1=xr[:, bass.ds(j, 1), 0:D].rearrange("p a n -> p (a n)"),
                                         op0=ALU.mult, op1=ALU.add).then_inc(res_ok, 1)
                dve.wait_ge(res_ok, j + 1)
                link3(dve.bn_stats(st3[:, k, :], res[:, k, :]))

            def norm3(m):
                s = [st3[:, 0:m, f] for f in range(6)]
                link3(dve.tensor_tensor(agg[:, 0, 0:m], s[1], s[4], ALU.subtract))
                link3(dve.tensor_tensor(agg[:, 1, 0:m], s[1], s[4], ALU.add))
                link3(dve.tensor_scalar(mv3[:, 0, 0:m], agg[:, 1, 0:m], 0.5, None, ALU.mult))
                link3(dve.scalar_tensor_tensor(out=agg[:, 2, 0:m], in0=agg[:, 0, 0:m], scalar=0.25 * D,
                                               in1=agg[:, 0, 0:m], op0=ALU.mult, op1=ALU.mult))
                link3(dve.tensor_tensor(agg[:, 3, 0:m], s[2], s[5], ALU.add))
                link3(dve.tensor_tensor(agg[:, 4, 0:m], agg[:, 2, 0:m], agg[:, 3, 0:m], ALU.add))
                link3(dve.tensor_scalar(mv3[:, 1, 0:m], agg[:, 4, 0:m], 1.0 / D, None, ALU.mult))
                newton(mv3[:, 1, 0:m], mv3[:, 0, 0:m], m, rstd3[:, 0:m], shift3[:, 0:m], linked=link3)

            def apply(j, k):
                dve.tensor_copy(token[:, k:k + 1],
                                xr[:, bass.ds(j, 1), D + 1:ROW].rearrange("p a n -> p (a n)").bitcast(I32)).then_inc(y_ok, 1)
                dve.tensor_scalar(y_out[:, k, :], res[:, k, :], rstd3[:, k:k + 1], shift3[:, k:k + 1],
                                  ALU.mult, ALU.add).then_inc(y_ok, 1)

            loop_links = [0]
            start3 = [before_loop]

            def link3(ins):
                loop_links[0] += 1
                ins.then_inc(dve_s, 1)
                dve.wait_ge(dve_s, start3[0] + loop_links[0])

            fetch_w1(0, 0)
            fetch_w1(1, 1)
            for k in range(U):
                fetch_w1(k + 2, (k + 2) % U)
                dve.wait_ge(xr_in[k // 2], 16)
                residual(k, k, 0)
            norm3(U)
            per_group = loop_links[0]

            def group(i, first=False):
                loop_links[0] = 0
                start3[0] = i * per_group + before_loop
                for k in range(U):
                    if not first:
                        dve.wait_ge(out_in[k], i * 16 - 16)
                    apply(i * U + k - U, k)
                    fetch_w1(i * U + k + 2, (k + 2) % U)
                    dve.wait_ge(xr_in[k // 2], i * 16 + 16)
                    dve.wait_ge(y_ok, (i * U + k - U) * 2 + 2)
                    residual(i * U + k, k, i)
                norm3(U)

            group(1, first=True)
            with dve.Fori(2, MAXP // U) as i:
                group(i)
            n = MAXP // U
            loop_links[0] = 0
            start3[0] = n * per_group + before_loop
            for k in range(U):
                dve.wait_ge(out_in[k], 16 * (n - 1))
                apply(U * (n - 1) + k, k)
            dve.wait_ge(y_ok, 2 * U * n)
            dve.wait_ge(xr_in[0], 16 * (n + 1))
            residual(MAXP - 1, 0, n)
            norm3(1)
            dve.wait_ge(out_in[0], 16 * n)
            apply(MAXP - 1, 0)

        @block.tensor
        def _(pe):
            def mm(o, l, r, start=True, stop=True):
                return pe.matmul(o, l, r, start=start, stop=stop)

            def tr_x(c):
                pe.wait_ge(xn_ok, C * c + C)
                if c:
                    pe.wait_ge(xt_ok, c)
                for i in range(C):
                    last = pe.transpose(ps_t[:, i, :], xn[:, C * c + i, :], ident[:])
                last.then_inc(xt_ps, 1)

            def proj_q(c):
                pe.wait_ge(xt_ok, c + 1)
                if c:
                    pe.wait_ge(q_act, 2 * c)
                mm(ps_q[:], wqkv_sb[:, 0:D], xn_t[:, C * c:C * c + C, :].rearrange("p i n -> p (i n)")).then_inc(q_ps, 1)

            def proj_kv(c):
                if c:
                    pe.wait_ge(v_ok, c)
                    pe.wait_ge(k_act, 2 * c)
                for i in range(C):
                    last = mm(ps_kv[:, i, :], xn_t[:, C * c + i, :], wqkv_sb[:, D:3 * D])
                last.then_inc(kv_ps, 1)

            def sum_kv(b):
                if b:
                    pe.wait_ge(kvh_ok, 2 * b)
                for c in range(CB * b, CB * b + CB):
                    pe.wait_ge(k_ok, c + 1)
                    pe.wait_ge(v_ok, c + 1)
                    for t in range(C * c, C * c + C):
                        last = mm(ps_kvh, k_sb[:, t, :], v_sb[:, t, :], t % JB == 0, t % JB == JB - 1)
                last.then_inc(kvh_ps, 1)

            def num(c):
                pe.wait_ge(kvh_ok, 2 * (c // CB) + 2)
                pe.wait_ge(q_ok, c + 1)
                if c:
                    pe.wait_ge(att_ok, 2 * c)
                for i in range(C):
                    last = mm(num_v[:, i // 2, i % 2, :], q_t[:, C * c + i, :], kv_h[:, c // CB, :])
                last.then_inc(num_ps, 1)

            def tr_att(c):
                pe.wait_ge(att_ok, 2 * c + 2)
                if c:
                    pe.wait_ge(pre_ok, c)
                for i in range(C):
                    last = pe.transpose(ps_o[:, i, :], att[:, C * c + i, :], ident[:])
                last.then_inc(at_ps, 1)

            def proj_out(c):
                pe.wait_ge(at_ok, c + 1)
                for i in range(C):
                    last = mm(ps_o[:, i, :], att_t[:, C * c + i, :], wout_sb[:])
                last.then_inc(wo_ps, 1)

            def tr_x1(c):
                pe.wait_ge(x1_ok, c + 1)
                pe.wait_ge(xt_ok, NC)
                if c:
                    pe.wait_ge(x1t_ok, c)
                for i in range(C):
                    last = pe.transpose(ps_t[:, i, :], rows[:, C * c + i, 0:D], ident[:])
                last.then_inc(x1t_ps, 1)

            def logits(c):
                pe.wait_ge(x1t_ok, c + 1)
                if c == 0:
                    pe.wait_ge(q_act, 2 * NC)
                elif c == 1:
                    pe.wait_ge(k_act, 2 * NC)
                    pe.wait_ge(v_ok, NC)
                else:
                    pe.wait_ge(below_ok, c - 1)
                for i in range(C):
                    last = mm(ps_lg(c)[:, i, :], x1_t[:, C * c + i, :], rw_sb[:])
                last.then_inc(lg_ps, 1)

            def ranks(c):
                pe.wait_ge(chosen_ok, c + 1)
                if c == 0:
                    pe.wait_ge(kvh_ok, 2 * B)
                elif c >= 2:
                    pe.wait_ge(slot_ok, c - 1)
                rk = ps_rk(c)
                mm(rk, before[:], chosen[:, c, :, :], True, False)
                for i in range(C):
                    last = mm(rk[:, i + 1:C + 1, :], ones[:],
                              chosen[:, c, i:i + 1, :].to_broadcast([P, C - i, E]), False, i == C - 1)
                last.then_inc(rk_ps, 1)

            pe.wait_ge(pool_c, P_IDENT)
            pe.wait_ge(vec_in, 48)
            pe.transpose(ps_vec, vec_rows[:], ident[0:E * FC + 2, 0:E * FC + 2]).then_inc(vec_ps, 1)
            tr_x(0)
            pe.wait_ge(wqkv_in, 16)
            proj_q(0)
            proj_kv(0)
            tr_x(1)
            proj_q(1)
            proj_kv(1)
            pe.wait_ge(v_ones, 1)
            pe.wait_ge(vec_ok, 1)
            sum_kv(0)
            tr_x(2)
            proj_q(2)
            num(0)
            proj_kv(2)
            tr_att(0)
            num(1)
            pe.wait_ge(wout_in, 16)
            proj_out(0)
            tr_x(3)
            tr_att(1)
            proj_q(3)
            proj_out(1)
            tr_x1(0)
            proj_kv(3)
            pe.wait_ge(rw_in, 16)
            logits(0)
            tr_x1(1)
            sum_kv(1)
            pe.wait_ge(pool_c, P_ONES)
            pe.wait_ge(consts_ok, N_CONSTS)
            ranks(0)
            logits(1)
            num(2)
            ranks(1)
            tr_att(2)
            num(3)
            proj_out(2)
            tr_att(3)
            proj_out(3)
            tr_x1(2)
            logits(2)
            tr_x1(3)
            ranks(2)
            logits(3)
            ranks(3)
            pe.wait_ge(own_ok, 1)
            mm(ps_row, own_sum[:], ident[:, 0:32]).then_inc(row_ps, 1)

            def turn(k):
                pe.transpose(ps_xt[k % 2], xs[:, k, :], ident[:]).then_inc(px_ps, 1)

            def hidden(j, k):
                pe.wait_ge(px_ok, j + 1)
                pe.wait_ge(w1_ok, j + 1)
                for c in range(FC):
                    last = mm(ps_h[k % 2][:, c, :], w1_cur[:, k, c * P:(c + 1) * P], xs_t[:, k, :])
                last.then_inc(h_ps, 1)

            def output(j, k):
                e = pe.value_load(page_e[0:1, bass.ds(j, 1)], min_val=0, max_val=E - 1)
                pe.wait_ge(hid_ok, 2 * j + 2)
                for c in range(FC):
                    mm(ps_y[k % 2], hid[:, k, c, :], w2_sb[:, bass.ds(e, 1), c, :].rearrange("p a n -> p (a n)"), c == 0, False)
                mm(ps_y[k % 2], ones[:], b2_k[:, bass.ds(e * D, D)], False, True).then_inc(y_ps, 1)

            pe.wait_ge(page_e_ok, 1)
            pe.wait_ge(w2_in, 16)
            pe.wait_ge(b2k_in, 48)
            pe.wait_ge(x1t_ok, NC)
            pe.wait_ge(xs_in[0], 16)
            turn(0)
            turn(1)
            hidden(0, 0)
            with pe.Fori(0, (NPG - 2) // U) as i:
                for k in range(U):
                    k2 = (k + 2) % U
                    pe.wait_ge(xs_in[k2 // 2], (i + (1 if k >= 2 else 0)) * 16 + 16)
                    pe.wait_ge(px_ok, i * U + k + 1)
                    turn(k2)
                    hidden(i * U + k + 1, (k + 1) % U)
                    output(i * U + k, k)
            pe.wait_ge(res_ok, MAXP - 2)
            output(MAXP - 1, 0)


INPUTS = ["L0_attn_x", "L0_attn_gamma", "L0_attn_beta", "L0_attn_Wqkv", "L0_attn_Wout", "L0_ffn_router_w",
          "L0_ffn_w1", "L0_ffn_b1", "L0_ffn_w2", "L0_ffn_b2"]


def kernel(**inputs):
    import numpy as np
    import concourse.bacc as bacc
    from concourse.bass_utils import run_bass_kernel_spmd

    nc = bacc.Bacc("TRN2", target_bir_lowering=False, num_devices=1)
    arrays, args = {}, []
    for name in INPUTS:
        arrays[name] = np.ascontiguousarray(inputs[name])
        args.append(nc.dram_tensor(name, arrays[name].shape, F32, kind="ExternalInput").ap())
    out = nc.dram_tensor("out", arrays["L0_attn_x"].shape, F32, kind="ExternalOutput").ap()
    build(nc, *args, out)
    result = run_bass_kernel_spmd(nc, [arrays], core_ids=[0])
    return result.results[0]["out"]
```

```python
from contextlib import ExitStack

import concourse.bass as bass
from concourse import mybir

F32 = mybir.dt.float32
BF16 = mybir.dt.bfloat16
I32 = mybir.dt.int32
ALU = mybir.AluOpType
ACT = mybir.ActivationFunctionType
AX = mybir.AxisListType.X

P = 128
D = 128
H, HD = 16, 8
E, F = 14, 256
B, S = 2, 1024
NT = B * S // P
C = 4
NC = NT // C
CB = NC // B
JB = S // P
FC = F // P
MAXP = (B * S - E) // P + E
NPG = 30
ROW = D + 2
WB = F + FC
LN_EPS = 1e-5
DENOM_EPS = 1e-6
NOWHERE = 4096
U = 4
KNOWN = "owners() gives an expert's number, or 0 for a page that nobody has"
assert MAXP == 29 and (NPG - 2) % U == 0


def build(nc, x, gamma, beta, wqkv, wout, router_w, w1, b1, w2, b2, out):
    with ExitStack() as ctx:
        def sb(name, shape, dt=F32):
            return ctx.enter_context(nc.sbuf_tensor(name, shape, dt))

        def ps(name, shape):
            return ctx.enter_context(nc.psum_tensor(name, shape, F32))

        def sem(name):
            return ctx.enter_context(nc.semaphore(name))

        pages = nc.dram_tensor("pages", [NPG * P, ROW], F32, kind="Internal").ap()
        out_rows = out.rearrange("b s d -> (b s) d")

        ident = sb("ident", [P, P])
        before = sb("before", [P, P], BF16)
        ones = sb("ones", [P, P], BF16)
        head_mask = sb("head_mask", [P, H])
        prio_i = sb("prio_i", [P, E], I32)
        prio = sb("prio", [P, E])
        eidx_i = sb("eidx_i", [P, E], I32)
        eidx = sb("eidx", [P, E])
        pidx_i = sb("pidx_i", [P, 1], I32)
        pidx = sb("pidx", [P, 1])
        empty_row = sb("empty_row", [P, ROW])
        wqkv_sb = sb("wqkv_sb", [P, 3 * D])
        wout_sb = sb("wout_sb", [P, D])
        rw_sb = sb("rw_sb", [P, E])
        vec_rows = sb("vec_rows", [E * FC + 2, P])
        vec_cols = sb("vec_cols", [P, E * FC + 2])
        w1_sb = sb("w1_sb", [P, E, WB])
        w2_sb = sb("w2_sb", [P, E, FC, D])
        b2_rows = sb("b2_rows", [E, D])
        b2_rest = sb("b2_rest", [E, 2, D])
        b2_part = sb("b2_part", [E, 3, D], BF16)
        b2_k = sb("b2_k", [P, E * D], BF16)

        x_sb = sb("x_sb", [P, NT, D])
        stats = sb("stats", [P, NT, 6])
        mv = sb("mv", [P, NT, 2])
        stats2 = sb("stats2", [P, NT, 6])
        mv2 = sb("mv2", [P, NT, 2])
        ve = sb("ve", [P, NT])
        ve2 = sb("ve2", [P, NT])
        rstd = sb("rstd", [P, NT])
        shift = sb("shift", [P, NT])
        rstd2 = sb("rstd2", [P, NT])
        exponent = sb("exponent", [P, C])
        xn = sb("xn", [P, NT, D])
        xn_t = sb("xn_t", [P, NT, P])
        q_exp = sb("q_exp", [P, NT * P])
        q_pos = sb("q_pos", [P, NT * P])
        q_t = sb("q_t", [P, NT, P])
        k_parts = sb("k_parts", [P, 2 * NT, D])
        k_exp, k_pos = k_parts[:, 0:NT, :], k_parts[:, NT:2 * NT, :]
        k_sb = sb("k_sb", [P, NT, D])
        v_sb = sb("v_sb", [P, NT, D + 1])
        kv_h = sb("kv_h", [P, B, D + H])
        den = sb("den", [P, C, H])
        rden = sb("rden", [P, C, H])
        att = sb("att", [P, NT, D])
        att_t = sb("att_t", [P, NT, P])
        pre = sb("pre", [P, NT, D])
        rows = sb("rows", [P, NT, ROW])
        x1_t = sb("x1_t", [P, NT, P])

        top = sb("top", [P, NT])
        is_top = sb("is_top", [P, C, E])
        ranked = sb("ranked", [P, C, E])
        first = sb("first", [P, NT])
        chosen = sb("chosen", [P, NC, C + 1, E], BF16)
        below = sb("below", [P, NT, E])
        e_exp = sb("e_exp", [P, NT, E])
        e_sum = sb("e_sum", [P, NT])
        cnt = sb("cnt", [P, NC + 1, E])
        cap = sb("cap", [P, NC + 1, E])
        base = sb("base", [P, NC + 1, E])
        used = sb("used", [P, NC + 1])
        cnt_i = sb("cnt_i", [P, E], I32)
        pg_i = sb("pg_i", [P, E], I32)
        LEAD = 8
        pages_had = sb("pages_had", [P, NC + 1, E])
        fresh = sb("fresh", [P, LEAD + E])
        pref = sb("pref", [P, 4, LEAD + E])
        start_pg = sb("start_pg", [P, NC, E])
        end_pg = sb("end_pg", [P, NC, E])
        open_pg = sb("open_pg", [P, E])
        jump = sb("jump", [P, E])
        gets = sb("gets", [P, E])
        room = sb("room", [P, E])
        low = sb("low", [P, E])
        over = sb("over", [P, C, E])
        slot_a = sb("slot_a", [P, C, E])
        slot_b = sb("slot_b", [P, C, E])
        slot_c = sb("slot_c", [P, C, E])
        slot_d = sb("slot_d", [P, C, E])
        slot = sb("slot", [P, NT], I32)
        own_a = sb("own_a", [P, NC, E])
        own_b = sb("own_b", [P, NC, E])
        own_c = sb("own_c", [P, NC, E])
        own_sum = sb("own_sum", [P, 1])
        page_e = sb("page_e", [1, 32], I32)
        page_e2 = sb("page_e2", [1, 32], I32)

        xs = sb("xs", [P, U, D])
        xr = sb("xr", [P, NPG, ROW])
        xs_t = sb("xs_t", [P, U, P])
        w1_cur = sb("w1_cur", [P, U, WB])
        hid = sb("hid", [P, U, FC, P])
        res = k_parts[:, 0:NPG, :]
        st3 = sb("st3", [P, U, 6])
        mv3 = sb("mv3", [P, U, 2])
        ve3 = sb("ve3", [P, U])
        rstd3 = sb("rstd3", [P, U])
        token = sb("token", [P, U], I32)
        y_out = sb("y_out", [P, U, D])
        spare = sb("spare", [P, 1])

        ps_t = ps("ps_t", [P, C, P])
        ps_q = ps("ps_q", [P, C * P])
        ps_kv = ps("ps_kv", [P, C, 2 * D])
        ps_acc = ps("ps_acc", [P, 512])
        ps_num = ps("ps_num", [P, 2, 512])
        ps_o = ps("ps_o", [P, C, P])
        ps_kvh = ps_acc[:, 0:D + 1]
        ps_vec = ps_acc[:, 0:E * FC + 2]
        num_v = ps_num[:, :, 0:2 * (D + H)].rearrange("p b (i n) -> p b i n", i=2)

        def ps_lg(c):
            bank = ps_kv[:, 0, :] if c % 2 else ps_q
            return bank[:, 0:C * E].rearrange("p (i e) -> p i e", e=E)

        def ps_rk(c):
            bank = ps_kv[:, 2, :] if c % 2 else ps_acc
            return bank[:, 0:(C + 1) * E].rearrange("p (i e) -> p i e", e=E)

        ps_row = ps_acc[0:1, 0:34]
        ps_xt = [ps_t[:, 0, :], ps_q[:, 0:P]]
        ps_h = [ps_kv[:, 0, :].rearrange("p (c n) -> p c n", c=FC), ps_kv[:, 2, :].rearrange("p (c n) -> p c n", c=FC)]
        ps_y = [ps_num[:, 0, 0:D], ps_num[:, 1, 0:D]]

        x_in = [sem(f"x_in{c}") for c in range(NC)]
        vec_in, wqkv_in, wout_in, rw_in = sem("vec_in"), sem("wqkv_in"), sem("wout_in"), sem("rw_in")
        w1_in, w2_in, b2_in, b2k_in = sem("w1_in"), sem("w2_in"), sem("b2_in"), sem("b2k_in")
        pages_clear = sem("pages_clear")
        pool_c = sem("pool_c")
        v_ones = sem("v_ones")
        vec_ps, vec_ok, b1_ok = sem("vec_ps"), sem("vec_ok"), sem("b1_ok")
        consts_ok = sem("consts_ok")
        b2_split, b2k_zero = sem("b2_split"), sem("b2k_zero")
        dve_s = sem("dve_s")
        ve_ok, rstd_ok = sem("ve_ok"), sem("rstd_ok")
        ve2_ok, rstd2_ok = sem("ve2_ok"), sem("rstd2_ok")
        ve3_ok, rstd3_ok = sem("ve3_ok"), sem("rstd3_ok")
        shift_ok = sem("shift_ok")
        xn_ok = sem("xn_ok")
        xt_ps, xt_ok = sem("xt_ps"), sem("xt_ok")
        q_ps, kv_ps = sem("q_ps"), sem("kv_ps")
        q_act, k_act, v_ok = sem("q_act"), sem("k_act"), sem("v_ok")
        q_ok, k_ok = sem("q_ok"), sem("k_ok")
        kvh_ps, kvh_ok = sem("kvh_ps"), sem("kvh_ok")
        num_ps, att_ok = sem("num_ps"), sem("att_ok")
        at_ps, at_ok = sem("at_ps"), sem("at_ok")
        wo_ps, pre_ok = sem("wo_ps"), sem("pre_ok")
        x1_ok, x1t_ps, x1t_ok = sem("x1_ok"), sem("x1t_ps"), sem("x1t_ok")
        lg_ps, chosen_ok, below_ok, eexp_ok = sem("lg_ps"), sem("chosen_ok"), sem("below_ok"), sem("eexp_ok")
        weight_ok = sem("weight_ok")
        rk_ps, slot_ok = sem("rk_ps"), sem("slot_ok")
        rows_out = sem("rows_out")
        own_ok, row_ps, page_e_ok = sem("own_ok"), sem("row_ps"), sem("page_e_ok")
        xs_in = [sem(f"xs_in{i}") for i in range(2)]
        xr_in = [sem(f"xr_in{i}") for i in range(2)]
        px_ps, px_ok = sem("px_ps"), sem("px_ok")
        w1_ok, h_ps, hid_ok, y_ps, res_ok = sem("w1_ok"), sem("h_ps"), sem("hid_ok"), sem("y_ps"), sem("res_ok")
        y_ok, st3_ok, mv3_ok = sem("y_ok"), sem("st3_ok"), sem("mv3_ok")
        out_in = [sem(f"out_in{k}") for k in range(U)]

        block = ctx.enter_context(nc.Block())

        N_CONSTS = 11
        (P_IDENT0, P_IDENT, P_BEF0, P_BEFORE, P_ONES, P_HM0, P_HM1, P_HEAD, P_PRIO, P_EIDX, P_PIDX, P_EMPTY0,
         P_EMPTY, P_TOKENS, P_EXPONENT) = range(1, 16)

        @block.sync
        def _(sp):
            def load_x(c):
                b, h = c // CB, c % CB
                src = x[b].rearrange("(p j) d -> p j d", j=JB)[:, C * h:C * h + C, :]
                sp.dma_start(x_sb[:, C * c:C * c + C, :], src).then_inc(x_in[c], 16)

            load_x(0)
            load_x(1)
            load_x(2)
            load_x(3)
            sp.dma_start(wout_sb[:], wout).then_inc(wout_in, 16)
            sp.dma_start(rw_sb[:], router_w).then_inc(rw_in, 16)
            sp.wait_ge(pool_c, P_EMPTY)
            sp.dma_start(pages.rearrange("(j p) d -> p j d", p=P),
                         empty_row[:].unsqueeze(1).to_broadcast([P, NPG, ROW])).then_inc(pages_clear, 16)
            sp.dma_start(w1_sb[:, :, 0:F], w1.rearrange("e d f -> d e f")).then_inc(w1_in, 16)
            sp.dma_start(w2_sb[:], w2.rearrange("e (c f) d -> f e c d", f=P)).then_inc(w2_in, 16)
            sp.wait_ge(b2_split, 1)
            sp.wait_ge(b2k_zero, 1)
            for i in range(3):
                sp.dma_start(b2_k[i:i + 1, :], b2_part[:, i, :]).then_inc(b2k_in, 16)

            def load_pair(q, half, ring_free=None, seen=None):
                if ring_free is not None:
                    sp.wait_ge(px_ps, ring_free)
                    sp.wait_ge(xr_in[half], seen)
                src = pages[bass.ds(q * (2 * P), 2 * P), :].rearrange("(j p) d -> p j d", p=P)
                sp.dma_start(xs[:, 2 * half:2 * half + 2, :], src[:, :, 0:D]).then_inc(xs_in[half], 16)
                sp.dma_start(xr[:, bass.ds(q * 2, 2), :], src).then_inc(xr_in[half], 16)

            sp.wait_ge(rows_out, 16 * NT)
            load_pair(0, 0)
            load_pair(1, 1)
            with sp.Fori(0, (NPG - 4) // U) as i:
                load_pair(2 * i + 2, 0, ring_free=4 * i + 2, seen=16 * i + 16)
                load_pair(2 * i + 3, 1, ring_free=4 * i + 4, seen=16 * i + 16)
            load_pair(NPG // 2 - 1, 0, ring_free=NPG - 4, seen=16 * (NPG // 4))
            for k in range(U):
                sp.wait_ge(out_in[k], 16 * ((MAXP - 1) // U + (1 if k == 0 else 0)))

        @block.gpsimd
        def _(pool):
            pool.memset(ident[:], 0.0).then_inc(pool_c, 1)
            pool.wait_ge(pool_c, P_IDENT0)
            pool.affine_select(out=ident[:], in_=ident[:], compare_op=ALU.not_equal, fill=1.0, base=0,
                               pattern=[[-1, P]], channel_multiplier=1).then_inc(pool_c, 1)
            pool.memset(before[:], 1.0).then_inc(pool_c, 1)
            pool.wait_ge(pool_c, P_BEF0)
            pool.affine_select(out=before[:], in_=before[:], compare_op=ALU.is_gt, fill=0.0, base=0,
                               pattern=[[1, P]], channel_multiplier=-1).then_inc(pool_c, 1)
            pool.memset(ones[:], 1.0).then_inc(pool_c, 1)
            pool.memset(head_mask[:], 1.0).then_inc(pool_c, 1)
            pool.wait_ge(pool_c, P_HM0)
            pool.affine_select(out=head_mask[:], in_=head_mask[:], compare_op=ALU.is_ge, fill=0.0, base=0,
                               pattern=[[-HD, H]], channel_multiplier=1).then_inc(pool_c, 1)
            pool.wait_ge(pool_c, P_HM1)
            pool.affine_select(out=head_mask[:], in_=head_mask[:], compare_op=ALU.is_ge, fill=0.0, base=HD - 1,
                               pattern=[[HD, H]], channel_multiplier=-1).then_inc(pool_c, 1)
            pool.iota(prio_i[:], pattern=[[-1, E]], base=E, channel_multiplier=0).then_inc(pool_c, 1)
            pool.iota(eidx_i[:], pattern=[[1, E]], base=0, channel_multiplier=0).then_inc(pool_c, 1)
            pool.iota(pidx_i[:], pattern=[[1, 1]], base=0, channel_multiplier=1).then_inc(pool_c, 1)
            pool.memset(empty_row[:, 0:D + 1], 0.0).then_inc(pool_c, 1)
            pool.iota(empty_row[:, D + 1:ROW].bitcast(I32), pattern=[[1, 1]], base=NOWHERE,
                      channel_multiplier=1).then_inc(pool_c, 1)
            for b in range(B):
                t = pool.iota(rows[:, b * JB:(b + 1) * JB, D + 1].bitcast(I32), pattern=[[1, JB]], base=b * S,
                              channel_multiplier=JB)
            t.then_inc(pool_c, 1)
            pool.memset(v_sb[:, :, D:D + 1], 1.0).then_inc(v_ones, 1)
            pool.memset(exponent[:], -0.5).then_inc(pool_c, 1)

            def power(out_, in_, done):
                pool.tensor_tensor(out_, in_, exponent[:, 0:in_.shape[1]], ALU.pow).then_inc(done, 1)

            def rstd_1(c):
                pool.wait_ge(ve_ok, c + 1)
                power(rstd[:, C * c:C * c + C], ve[:, C * c:C * c + C], rstd_ok)

            def rstd_2(c):
                pool.wait_ge(ve2_ok, c + 1)
                power(rstd2[:, C * c:C * c + C], ve2[:, C * c:C * c + C], rstd2_ok)

            def norm1(c):
                pool.wait_ge(x_in[c], 16)
                pool.wait_ge(shift_ok, c)
                for t in range(C * c, C * c + C):
                    pool.tensor_scalar(xn[:, t, :], x_sb[:, t, :], rstd[:, t:t + 1], shift[:, t:t + 1],
                                       ALU.mult, ALU.add).then_inc(xn_ok, 1)

            pool.wait_ge(pool_c, P_EXPONENT)
            rstd_1(0)
            rstd_1(1)
            norm1(1)
            rstd_1(2)
            norm1(2)
            rstd_1(3)
            norm1(3)
            last_slot = pool.to_reg(NPG * P - 1)

            def scatter(c):
                pool.wait_ge(x1_ok, c + 1)
                pool.wait_ge(weight_ok, c + 1)
                pool.wait_ge(slot_ok, c + 1)
                for t in range(C * c, C * c + C):
                    pool.indirect_dma_start(pages, bass.IndirectOffsetOnAxis(ap=slot[:, t:t + 1], axis=0),
                                            rows[:, t, :], None, bounds_check=last_slot,
                                            oob_is_err=False).then_inc(rows_out, 16)

            rstd_2(0)
            rstd_2(1)
            pool.wait_ge(pages_clear, 16)
            pool.wait_ge(pool_c, P_TOKENS)
            scatter(0)
            rstd_2(2)
            scatter(1)
            rstd_2(3)
            scatter(2)
            scatter(3)

            last_token = pool.to_reg(B * S - 1)

            wanted = pool.alloc_register("wanted")
            pool.reg_mov(wanted, 0)

            def store(k):
                pool.reg_add(wanted, wanted, 2)
                pool.wait_ge(page_e_ok, 1)
                pool.wait_ge(y_ok, wanted)
                pool.indirect_dma_start(out_rows, bass.IndirectOffsetOnAxis(ap=token[:, k:k + 1], axis=0),
                                        y_out[:, k, :], None, bounds_check=last_token,
                                        oob_is_err=False).then_inc(out_in[k], 16)

            def rstd_3(n):
                pool.reg_add(groups, groups, 1)
                pool.wait_ge(page_e_ok, 1)
                pool.wait_ge(ve3_ok, groups)
                power(rstd3[:, 0:n], ve3[:, 0:n], rstd3_ok)

            groups = pool.alloc_register("groups")
            pool.reg_mov(groups, 0)
            with pool.Fori(0, MAXP // U):
                rstd_3(U)
                for k in range(U):
                    store(k)
            rstd_3(1)
            store(0)

        @block.scalar
        def _(act):
            act.dma_start(vec_rows[0:E * FC, :], b1.rearrange("e (c f) -> (e c) f", c=FC)).then_inc(vec_in, 16)
            act.dma_start(vec_rows[E * FC:E * FC + 1, :], gamma.rearrange("(a d) -> a d", a=1)).then_inc(vec_in, 16)
            act.dma_start(vec_rows[E * FC + 1:E * FC + 2, :], beta.rearrange("(a d) -> a d", a=1)).then_inc(vec_in, 16)
            act.dma_start(wqkv_sb[:], wqkv).then_inc(wqkv_in, 16)
            act.dma_start(b2_rows[:], b2).then_inc(b2_in, 16)

            def xt(c):
                act.wait_ge(xt_ps, c + 1)
                act.activation(xn_t[:, C * c:C * c + C, :], ps_t[:], ACT.Identity, bias=vec_cols[:, E * FC + 1:E * FC + 2],
                               scale=vec_cols[:, E * FC:E * FC + 1]).then_inc(xt_ok, 1)

            def q(c):
                act.wait_ge(q_ps, c + 1)
                act.activation(q_exp[:, c * C * P:(c + 1) * C * P], ps_q[:], ACT.Exp).then_inc(q_act, 1)
                act.activation(q_pos[:, c * C * P:(c + 1) * C * P], ps_q[:], ACT.Relu).then_inc(q_act, 1)

            def kv(c):
                act.wait_ge(kv_ps, c + 1)
                act.activation(k_exp[:, C * c:C * c + C, :], ps_kv[:, :, 0:D], ACT.Exp).then_inc(k_act, 1)
                act.activation(k_pos[:, C * c:C * c + C, :], ps_kv[:, :, 0:D], ACT.Relu).then_inc(k_act, 1)
                act.copy(v_sb[:, C * c:C * c + C, 0:D], ps_kv[:, :, D:2 * D]).then_inc(v_ok, 1)

            def at(c):
                act.wait_ge(at_ps, c + 1)
                act.copy(att_t[:, C * c:C * c + C, :], ps_o[:]).then_inc(at_ok, 1)

            def x1t(c):
                act.wait_ge(x1t_ps, c + 1)
                act.copy(x1_t[:, C * c:C * c + C, :], ps_t[:]).then_inc(x1t_ok, 1)

            def eexp(c):
                act.wait_ge(below_ok, c + 1)
                act.activation(e_exp[:, C * c:C * c + C, :], below[:, C * c:C * c + C, :], ACT.Exp).then_inc(eexp_ok, 1)

            act.wait_ge(vec_ok, 1)
            xt(0)
            q(0)
            xt(1)
            kv(0)
            q(1)
            kv(1)
            xt(2)
            q(2)
            at(0)
            kv(2)
            at(1)
            xt(3)
            q(3)
            x1t(0)
            kv(3)
            x1t(1)
            eexp(0)
            at(2)
            eexp(1)
            at(3)
            x1t(2)
            x1t(3)
            eexp(2)
            eexp(3)

            def page_t(j, k):
                act.wait_ge(px_ps, j + 1)
                act.copy(xs_t[:, k, :], ps_xt[k % 2]).then_inc(px_ok, 1)

            def gelu(j, k):
                act.wait_ge(h_ps, j + 1)
                for c in range(FC):
                    act.activation(hid[:, k, c, :], ps_h[k % 2][:, c, :], ACT.Gelu,
                                   bias=w1_cur[:, k, F + c:F + c + 1]).then_inc(hid_ok, 1)

            act.preload_act_table(ACT.Gelu)
            page_t(0, 0)
            page_t(1, 1)
            gelu(0, 0)
            with act.Fori(0, (NPG - 2) // U) as i:
                for k in range(U):
                    page_t(U * i + k + 2, (k + 2) % U)
                    gelu(U * i + k + 1, (k + 1) % U)

        @block.vector
        def _(dve):
            links = [0]

            def link(ins):
                links[0] += 1
                ins.then_inc(dve_s, 1)
                dve.wait_ge(dve_s, links[0])

            def step(ins):
                links[0] += 1
                ins.then_inc(dve_s, 1)
                return links[0]

            def after(n):
                dve.wait_ge(dve_s, n)

            dve.wait_ge(pool_c, P_PIDX)
            dve.tensor_copy(prio[:], prio_i[:]).then_inc(consts_ok, 1)
            dve.tensor_copy(eidx[:], eidx_i[:]).then_inc(consts_ok, 1)
            dve.tensor_copy(pidx[:], pidx_i[:]).then_inc(consts_ok, 1)
            for z in (cnt, cap, base, pages_had):
                dve.memset(z[:, 0, :], 0.0).then_inc(consts_ok, 1)
            dve.memset(used[:, 0:1], 0.0).then_inc(consts_ok, 1)
            dve.memset(pref[:, :, 0:LEAD], 0.0).then_inc(consts_ok, 1)
            dve.memset(fresh[:, 0:LEAD], 0.0).then_inc(consts_ok, 1)
            dve.memset(chosen[:, :, C, :], 0.0).then_inc(consts_ok, 1)

            def stats1(c):
                dve.wait_ge(x_in[c], 16)
                ts = range(C * c, C * c + C)
                for t in ts:
                    last = dve.bn_stats(stats[:, t, :], x_sb[:, t, :])
                link(last)
                for t in ts:
                    last = dve.bn_aggr(mv[:, t, :], stats[:, t, :])
                link(last)
                dve.tensor_scalar(ve[:, C * c:C * c + C], mv[:, C * c:C * c + C, 1], LN_EPS, None,
                                  ALU.add).then_inc(ve_ok, 1)

            def shift1(c):
                o = slice(C * c, C * c + C)
                dve.wait_ge(rstd_ok, c + 1)
                dve.scalar_tensor_tensor(out=shift[:, o], in0=mv[:, o, 0], scalar=-1.0, in1=rstd[:, o],
                                         op0=ALU.mult, op1=ALU.mult).then_inc(shift_ok, 1)

            stats1(0)
            stats1(1)
            dve.wait_ge(rstd_ok, 1)
            for t in range(C):
                dve.tensor_scalar(xn[:, t, :], x_sb[:, t, :], mv[:, t, 0:1], rstd[:, t:t + 1],
                                  ALU.subtract, ALU.mult).then_inc(xn_ok, 1)
            shift1(1)
            dve.wait_ge(vec_ps, 1)
            dve.tensor_copy(vec_cols[:], ps_vec).then_inc(vec_ok, 1)
            stats1(2)
            dve.wait_ge(b2_in, 16)
            link(dve.tensor_copy(b2_part[:, 0, :], b2_rows[:]))
            link(dve.tensor_tensor(b2_rest[:, 0, :], b2_rows[:], b2_part[:, 0, :], ALU.subtract))
            link(dve.tensor_copy(b2_part[:, 1, :], b2_rest[:, 0, :]))
            link(dve.tensor_tensor(b2_rest[:, 1, :], b2_rest[:, 0, :], b2_part[:, 1, :], ALU.subtract))
            dve.tensor_copy(b2_part[:, 2, :], b2_rest[:, 1, :]).then_inc(b2_split, 1)
            dve.memset(b2_k[:].bitcast(I32), 0).then_inc(b2k_zero, 1)

            def elu_q(c):
                o = slice(c * C * P, (c + 1) * C * P)
                dve.wait_ge(q_act, 2 * c + 2)
                dve.scalar_tensor_tensor(out=q_t[:, C * c:C * c + C, :].rearrange("p i n -> p (i n)"), in0=q_exp[:, o],
                                         scalar=1.0, in1=q_pos[:, o], op0=ALU.min, op1=ALU.add).then_inc(q_ok, 1)

            def elu_k(c):
                o = slice(C * c, C * c + C)
                dve.wait_ge(k_act, 2 * c + 2)
                dve.scalar_tensor_tensor(out=k_sb[:, o, :], in0=k_exp[:, o, :], scalar=1.0, in1=k_pos[:, o, :],
                                         op0=ALU.min, op1=ALU.add).then_inc(k_ok, 1)

            def heads(b):
                dve.wait_ge(kvh_ps, b + 1)
                dve.wait_ge(pool_c, P_HEAD)
                dve.tensor_tensor(kv_h[:, b, 0:D].rearrange("p (h e) -> p h e", e=HD),
                                  ps_kvh[:, 0:D].rearrange("p (h e) -> p h e", e=HD),
                                  head_mask[:].unsqueeze(2).to_broadcast([P, H, HD]), ALU.mult).then_inc(kvh_ok, 1)
                dve.tensor_scalar(kv_h[:, b, D:D + H], head_mask[:], ps_kvh[:, D:D + 1], None,
                                  ALU.mult).then_inc(kvh_ok, 1)

            def divide(c):
                dve.wait_ge(num_ps, c + 1)
                link(dve.tensor_scalar(den[:].rearrange("p (b i) h -> p b i h", b=2), num_v[:, :, :, D:D + H],
                                       DENOM_EPS, None, ALU.add))
                link(dve.reciprocal(rden[:], den[:]))
                for b in range(2):
                    t = C * c + 2 * b
                    dve.tensor_tensor(att[:, t:t + 2, :].rearrange("p i (h e) -> p i h e", e=HD),
                                      num_v[:, b, :, 0:D].rearrange("p i (h e) -> p i h e", e=HD),
                                      rden[:, 2 * b:2 * b + 2, :].unsqueeze(3).to_broadcast([P, 2, H, HD]),
                                      ALU.mult).then_inc(att_ok, 1)

            def stats2_(c):
                ts = range(C * c, C * c + C)
                dve.wait_ge(wo_ps, c + 1)
                dve.scalar_tensor_tensor(out=pre[:, C * c:C * c + C, :], in0=x_sb[:, C * c:C * c + C, :], scalar=2.0,
                                         in1=ps_o[:], op0=ALU.mult, op1=ALU.add).then_inc(pre_ok, 1)
                dve.wait_ge(pre_ok, c + 1)
                for t in ts:
                    last = dve.bn_stats(stats2[:, t, :], pre[:, t, :])
                link(last)
                for t in ts:
                    last = dve.bn_aggr(mv2[:, t, :], stats2[:, t, :])
                link(last)
                dve.tensor_scalar(ve2[:, C * c:C * c + C], mv2[:, C * c:C * c + C, 1], LN_EPS, None,
                                  ALU.add).then_inc(ve2_ok, 1)

            def x1(c):
                dve.wait_ge(rstd2_ok, c + 1)
                for t in range(C * c, C * c + C):
                    last = dve.tensor_scalar(rows[:, t, 0:D], pre[:, t, :], mv2[:, t, 0:1], rstd2[:, t:t + 1],
                                             ALU.subtract, ALU.mult)
                last.then_inc(x1_ok, 1)

            def route(c):
                o = slice(C * c, C * c + C)
                lg = ps_lg(c)
                prio_b = prio[:].unsqueeze(1).to_broadcast([P, C, E])
                top_b = top[:, o].unsqueeze(2).to_broadcast([P, C, E])
                dve.wait_ge(lg_ps, c + 1)
                link(dve.tensor_reduce(top[:, o], lg, AX, ALU.max))
                link(dve.tensor_tensor(is_top[:], lg, top_b, ALU.is_equal))
                link(dve.tensor_tensor(ranked[:], is_top[:], prio_b, ALU.mult))
                link(dve.tensor_reduce(first[:, o], ranked[:], AX, ALU.max))
                dve.tensor_tensor(chosen[:, c, 0:C, :], prio_b, first[:, o].unsqueeze(2).to_broadcast([P, C, E]),
                                  ALU.is_equal).then_inc(chosen_ok, 1)
                dve.tensor_tensor(below[:, o, :], lg, top_b, ALU.subtract).then_inc(below_ok, 1)

            def weigh(c):
                o = slice(C * c, C * c + C)
                dve.wait_ge(eexp_ok, c + 1)
                link(dve.tensor_reduce(e_sum[:, o], e_exp[:, o, :], AX, ALU.add))
                dve.reciprocal(rows[:, o, D], e_sum[:, o]).then_inc(weight_ok, 1)

            def place(c):
                rk = ps_rk(c)

                def each(a):
                    return a.unsqueeze(1).to_broadcast([P, C, E])

                dve.tensor_tensor(room[:], cap[:, c, :], cnt[:, c, :], ALU.subtract)
                dve.tensor_tensor(low[:], base[:, c, :], cnt[:, c, :], ALU.add)
                ahead = step(dve.tensor_tensor(open_pg[:], base[:, c, :], cap[:, c, :], ALU.add))
                dve.wait_ge(rk_ps, c + 1)
                a = step(dve.scalar_tensor_tensor(out=cnt_i[:], in0=rk[:, C, :], scalar=float(P - 1),
                                                  in1=cnt[:, c, :], op0=ALU.add, op1=ALU.add))
                dve.tensor_tensor(cnt[:, c + 1, :], cnt[:, c, :], rk[:, C, :], ALU.add)
                after(a)
                a = step(dve.tensor_scalar(pg_i[:], cnt_i[:], 7, None, ALU.logical_shift_right))
                over_ = step(dve.tensor_tensor(over[:], rk[:, 0:C, :], each(room[:]), ALU.is_ge))
                after(a)
                a = step(dve.tensor_tensor(fresh[:, LEAD:], pg_i[:], pages_had[:, c, :], ALU.subtract))
                dve.tensor_copy(pages_had[:, c + 1, :], pg_i[:])
                after(a)
                src, b = fresh, None
                for s, d in enumerate((1, 2, 4, 8)):
                    a = step(dve.tensor_tensor(pref[:, s, LEAD:], src[:, LEAD:], src[:, LEAD - d:LEAD - d + E], ALU.add))
                    if s == 0:
                        b = step(dve.tensor_tensor(slot_b[:], rk[:, 0:C, :], each(low[:]), ALU.add))
                    if s == 1:
                        dve.tensor_scalar(cap[:, c + 1, :], pg_i[:], float(P), None, ALU.mult)
                    after(a)
                    src = pref[:, s]
                link(dve.scalar_tensor_tensor(out=start_pg[:, c, :], in0=src[:, LEAD:], scalar=used[:, c:c + 1],
                                              in1=fresh[:, LEAD:], op0=ALU.add, op1=ALU.subtract))
                a = step(dve.scalar_tensor_tensor(out=jump[:], in0=start_pg[:, c, :], scalar=float(P), in1=open_pg[:],
                                                  op0=ALU.mult, op1=ALU.subtract))
                dve.tensor_scalar(used[:, c + 1:c + 2], src[:, LEAD + E - 1:LEAD + E], used[:, c:c + 1], None, ALU.add)
                after(a)
                a = step(dve.tensor_tensor(slot_a[:], over[:], each(jump[:]), ALU.mult))
                g = step(dve.scalar_tensor_tensor(out=gets[:], in0=fresh[:, LEAD:], scalar=0.0, in1=jump[:],
                                                  op0=ALU.is_gt, op1=ALU.mult))
                after(a)
                a = step(dve.tensor_tensor(slot_c[:], slot_a[:], slot_b[:], ALU.add))
                after(g)
                dve.tensor_tensor(base[:, c + 1, :], base[:, c, :], gets[:], ALU.add)
                after(a)
                a = step(dve.tensor_tensor(slot_d[:], slot_c[:], chosen[:, c, 0:C, :], ALU.mult))
                step(dve.tensor_tensor(end_pg[:, c, :], start_pg[:, c, :], fresh[:, LEAD:], ALU.add))
                after(a)
                with nc.allow_low_precision(reason="slots are whole numbers below 2**24"):
                    dve.tensor_reduce(slot[:, C * c:C * c + C], slot_d[:], AX, ALU.add).then_inc(slot_ok, 1)

            def owners():
                link(dve.tensor_scalar(own_a[:], start_pg[:], pidx[:, 0:1], None, ALU.is_le))
                link(dve.tensor_scalar(own_b[:], end_pg[:], pidx[:, 0:1], None, ALU.is_gt))
                link(dve.tensor_tensor(own_c[:], own_a[:], own_b[:], ALU.mult))
                link(dve.tensor_tensor(own_a[:], own_c[:], eidx[:].unsqueeze(1).to_broadcast([P, NC, E]), ALU.mult))
                dve.tensor_reduce(own_sum[:], own_a[:].rearrange("p c e -> p (c e)"), AX, ALU.add).then_inc(own_ok, 1)

            shift1(2)
            elu_q(0)
            stats1(3)
            elu_k(0)
            shift1(3)
            elu_q(1)
            elu_k(1)
            dve.wait_ge(consts_ok, N_CONSTS)
            heads(0)
            divide(0)
            elu_q(2)
            divide(1)
            stats2_(0)
            elu_k(2)
            elu_q(3)
            x1(0)
            stats2_(1)
            elu_k(3)
            x1(1)
            route(0)
            heads(1)
            weigh(0)
            route(1)
            divide(2)
            place(0)
            weigh(1)
            divide(3)
            stats2_(2)
            place(1)
            x1(2)
            stats2_(3)
            route(2)
            x1(3)
            place(2)
            route(3)
            weigh(2)
            place(3)
            owners()
            weigh(3)
            dve.wait_ge(row_ps, 1)
            dve.tensor_copy(page_e[:], ps_row[:, 0:32]).then_inc(page_e_ok, 1)
            dve.tensor_copy(page_e2[:], ps_row[:, 2:34]).then_inc(page_e_ok, 1)
            dve.wait_ge(w1_in, 16)
            link(dve.tensor_copy(w1_sb[:, :, F:WB], vec_cols[:, 0:E * FC].rearrange("p (e c) -> p e c", c=FC)))
            dve.wait_ge(page_e_ok, 2)

            before_loop = links[0]

            def experts_of(row, j):
                return nc.values_load_multi_w_load_instructions(row[0:1, bass.ds(j, U)], engines=[dve.engine],
                                                                min_val=0, max_val=E - 1,
                                                                skip_runtime_bounds_check_because=KNOWN)[1]

            def fetch_w1(j, k, e):
                dve.tensor_copy(w1_cur[:, k, :],
                                w1_sb[:, bass.ds(e, 1), :].rearrange("p a n -> p (a n)")).then_inc(w1_ok, 1)

            def page(a, j):
                return a[:, bass.ds(j, 1), :].rearrange("p a n -> p (a n)")

            def residual(j, k):
                dve.wait_ge(y_ps, j + 1)
                dve.scalar_tensor_tensor(out=page(res, j), in0=ps_y[k % 2], scalar=page(xr, j)[:, D:D + 1],
                                         in1=page(xr, j)[:, 0:D], op0=ALU.mult, op1=ALU.add).then_inc(res_ok, 1)

            def apply(j, k):
                dve.tensor_scalar(y_out[:, k, :], page(res, j), mv3[:, k, 0:1], rstd3[:, k:k + 1],
                                  ALU.subtract, ALU.mult).then_inc(y_ok, 1)
                dve.tensor_copy(token[:, k:k + 1], page(xr, j)[:, D + 1:ROW].bitcast(I32)).then_inc(y_ok, 1)

            def stats3(j, k):
                dve.wait_ge(res_ok, j + 1)
                dve.memset(spare[:], 0.0)
                dve.bn_stats(st3[:, k, :], page(res, j)).then_inc(st3_ok, 1)
                dve.wait_ge(st3_ok, j + 1)
                dve.memset(spare[:], 0.0)
                dve.bn_aggr(mv3[:, k, :], st3[:, k, :]).then_inc(mv3_ok, 1)

            def variances(i, n):
                dve.wait_ge(mv3_ok, U * i + n)
                dve.tensor_scalar(ve3[:, 0:n], mv3[:, 0:n, 1], LN_EPS, None, ALU.add).then_inc(ve3_ok, 1)

            def group(i, applies=True, reuses=True):
                e = experts_of(page_e2, i * U)
                for k in range(U):
                    fetch_w1(i * U + k + 2, (k + 2) % U, e[k])
                    dve.wait_ge(xr_in[k // 2], i * 16 + 16)
                    residual(i * U + k, k)
                    if applies:
                        if k == 0:
                            dve.wait_ge(rstd3_ok, i)
                        if reuses:
                            dve.wait_ge(out_in[k], i * 16 - 16)
                        apply(i * U + k - U, k)
                    stats3(i * U + k, k)
                variances(i, U)

            e = experts_of(page_e, 0)
            fetch_w1(0, 0, e[0])
            fetch_w1(1, 1, e[1])
            group(0, applies=False)
            group(1, reuses=False)
            with dve.Fori(2, MAXP // U) as i:
                group(i)
            n = MAXP // U
            dve.wait_ge(rstd3_ok, n)
            for k in range(U):
                dve.wait_ge(out_in[k], 16 * (n - 1))
                apply(U * (n - 1) + k, k)
            dve.wait_ge(xr_in[0], 16 * (n + 1))
            residual(MAXP - 1, 0)
            stats3(MAXP - 1, 0)
            variances(n, 1)
            dve.wait_ge(out_in[0], 16 * n)
            dve.wait_ge(rstd3_ok, n + 1)
            apply(MAXP - 1, 0)

        @block.tensor
        def _(pe):
            def mm(o, l, r, start=True, stop=True):
                return pe.matmul(o, l, r, start=start, stop=stop)

            def tr_x(c):
                pe.wait_ge(xn_ok, C * c + C)
                if c:
                    pe.wait_ge(xt_ok, c)
                for i in range(C):
                    last = pe.transpose(ps_t[:, i, :], xn[:, C * c + i, :], ident[:])
                last.then_inc(xt_ps, 1)

            def proj_q(c):
                pe.wait_ge(xt_ok, c + 1)
                if c:
                    pe.wait_ge(q_act, 2 * c)
                mm(ps_q[:], wqkv_sb[:, 0:D], xn_t[:, C * c:C * c + C, :].rearrange("p i n -> p (i n)")).then_inc(q_ps, 1)

            def proj_kv(c):
                if c:
                    pe.wait_ge(v_ok, c)
                    pe.wait_ge(k_act, 2 * c)
                for i in range(C):
                    last = mm(ps_kv[:, i, :], xn_t[:, C * c + i, :], wqkv_sb[:, D:3 * D])
                last.then_inc(kv_ps, 1)

            def sum_kv(b):
                if b:
                    pe.wait_ge(kvh_ok, 2 * b)
                for c in range(CB * b, CB * b + CB):
                    pe.wait_ge(k_ok, c + 1)
                    pe.wait_ge(v_ok, c + 1)
                    for t in range(C * c, C * c + C):
                        last = mm(ps_kvh, k_sb[:, t, :], v_sb[:, t, :], t % JB == 0, t % JB == JB - 1)
                last.then_inc(kvh_ps, 1)

            def num(c):
                pe.wait_ge(kvh_ok, 2 * (c // CB) + 2)
                pe.wait_ge(q_ok, c + 1)
                if c:
                    pe.wait_ge(att_ok, 2 * c)
                for i in range(C):
                    last = mm(num_v[:, i // 2, i % 2, :], q_t[:, C * c + i, :], kv_h[:, c // CB, :])
                last.then_inc(num_ps, 1)

            def tr_att(c):
                pe.wait_ge(att_ok, 2 * c + 2)
                if c:
                    pe.wait_ge(pre_ok, c)
                for i in range(C):
                    last = pe.transpose(ps_o[:, i, :], att[:, C * c + i, :], ident[:])
                last.then_inc(at_ps, 1)

            def proj_out(c):
                pe.wait_ge(at_ok, c + 1)
                for i in range(C):
                    last = mm(ps_o[:, i, :], att_t[:, C * c + i, :], wout_sb[:])
                last.then_inc(wo_ps, 1)

            def tr_x1(c):
                pe.wait_ge(x1_ok, c + 1)
                pe.wait_ge(xt_ok, NC)
                if c:
                    pe.wait_ge(x1t_ok, c)
                for i in range(C):
                    last = pe.transpose(ps_t[:, i, :], rows[:, C * c + i, 0:D], ident[:])
                last.then_inc(x1t_ps, 1)

            def logits(c):
                pe.wait_ge(x1t_ok, c + 1)
                if c == 0:
                    pe.wait_ge(q_act, 2 * NC)
                elif c == 1:
                    pe.wait_ge(k_act, 2 * NC)
                    pe.wait_ge(v_ok, NC)
                else:
                    pe.wait_ge(below_ok, c - 1)
                for i in range(C):
                    last = mm(ps_lg(c)[:, i, :], x1_t[:, C * c + i, :], rw_sb[:])
                last.then_inc(lg_ps, 1)

            def ranks(c):
                pe.wait_ge(chosen_ok, c + 1)
                if c == 0:
                    pe.wait_ge(kvh_ok, 2 * B)
                elif c >= 2:
                    pe.wait_ge(slot_ok, c - 1)
                rk = ps_rk(c)
                mm(rk, before[:], chosen[:, c, :, :], True, False)
                for i in range(C):
                    last = mm(rk[:, i + 1:C + 1, :], ones[:],
                              chosen[:, c, i:i + 1, :].to_broadcast([P, C - i, E]), False, i == C - 1)
                last.then_inc(rk_ps, 1)

            pe.wait_ge(pool_c, P_IDENT)
            pe.wait_ge(vec_in, 48)
            pe.transpose(ps_vec, vec_rows[:], ident[0:E * FC + 2, 0:E * FC + 2]).then_inc(vec_ps, 1)
            tr_x(0)
            pe.wait_ge(wqkv_in, 16)
            proj_q(0)
            proj_kv(0)
            tr_x(1)
            proj_q(1)
            proj_kv(1)
            pe.wait_ge(v_ones, 1)
            pe.wait_ge(vec_ok, 1)
            sum_kv(0)
            tr_x(2)
            proj_q(2)
            num(0)
            proj_kv(2)
            tr_att(0)
            num(1)
            pe.wait_ge(wout_in, 16)
            proj_out(0)
            tr_x(3)
            tr_att(1)
            proj_q(3)
            proj_out(1)
            tr_x1(0)
            proj_kv(3)
            pe.wait_ge(rw_in, 16)
            logits(0)
            tr_x1(1)
            sum_kv(1)
            pe.wait_ge(pool_c, P_ONES)
            pe.wait_ge(consts_ok, N_CONSTS)
            ranks(0)
            logits(1)
            num(2)
            ranks(1)
            tr_att(2)
            num(3)
            proj_out(2)
            tr_att(3)
            proj_out(3)
            tr_x1(2)
            logits(2)
            tr_x1(3)
            ranks(2)
            logits(3)
            ranks(3)
            pe.wait_ge(own_ok, 1)
            mm(ps_row, own_sum[:], ident[:, 0:34]).then_inc(row_ps, 1)

            def turn(k):
                pe.transpose(ps_xt[k % 2], xs[:, k, :], ident[:]).then_inc(px_ps, 1)

            def hidden(j, k):
                pe.wait_ge(px_ok, j + 1)
                pe.wait_ge(w1_ok, j + 1)
                for c in range(FC):
                    last = mm(ps_h[k % 2][:, c, :], w1_cur[:, k, c * P:(c + 1) * P], xs_t[:, k, :])
                last.then_inc(h_ps, 1)

            def experts_of(j):
                return nc.values_load_multi_w_load_instructions(page_e[0:1, bass.ds(j, U)], engines=[pe.engine],
                                                                min_val=0, max_val=E - 1,
                                                                skip_runtime_bounds_check_because=KNOWN)[1]

            def output(j, k, e):
                pe.wait_ge(hid_ok, 2 * j + 2)
                for c in range(FC):
                    mm(ps_y[k % 2], hid[:, k, c, :], w2_sb[:, bass.ds(e, 1), c, :].rearrange("p a n -> p (a n)"), c == 0, False)
                mm(ps_y[k % 2], ones[:], b2_k[:, bass.ds(e * D, D)], False, True).then_inc(y_ps, 1)

            pe.wait_ge(page_e_ok, 1)
            pe.wait_ge(w2_in, 16)
            pe.wait_ge(b2k_in, 48)
            pe.wait_ge(x1t_ok, NC)
            pe.wait_ge(xs_in[0], 16)
            turn(0)
            turn(1)
            hidden(0, 0)
            with pe.Fori(0, (NPG - 2) // U) as i:
                e = experts_of(i * U)
                for k in range(U):
                    k2 = (k + 2) % U
                    pe.wait_ge(xs_in[k2 // 2], (i + (1 if k >= 2 else 0)) * 16 + 16)
                    pe.wait_ge(px_ok, i * U + k + 1)
                    turn(k2)
                    hidden(i * U + k + 1, (k + 1) % U)
                    output(i * U + k, k, e[k])
            pe.wait_ge(res_ok, MAXP - 2)
            output(MAXP - 1, 0, experts_of(MAXP - 1)[0])


INPUTS = ["L0_attn_x", "L0_attn_gamma", "L0_attn_beta", "L0_attn_Wqkv", "L0_attn_Wout", "L0_ffn_router_w",
          "L0_ffn_w1", "L0_ffn_b1", "L0_ffn_w2", "L0_ffn_b2"]


def kernel(**inputs):
    import numpy as np
    import concourse.bacc as bacc
    from concourse.bass_utils import run_bass_kernel_spmd

    nc = bacc.Bacc("TRN2", target_bir_lowering=False, num_devices=1)
    arrays, args = {}, []
    for name in INPUTS:
        arrays[name] = np.ascontiguousarray(inputs[name])
        args.append(nc.dram_tensor(name, arrays[name].shape, F32, kind="ExternalInput").ap())
    out = nc.dram_tensor("out", arrays["L0_attn_x"].shape, F32, kind="ExternalOutput").ap()
    build(nc, *args, out)
    result = run_bass_kernel_spmd(nc, [arrays], core_ids=[0])
    return result.results[0]["out"]
```

```python
from contextlib import ExitStack

import concourse.bass as bass
from concourse import mybir

F32 = mybir.dt.float32
BF16 = mybir.dt.bfloat16
I32 = mybir.dt.int32
ALU = mybir.AluOpType
ACT = mybir.ActivationFunctionType
AX = mybir.AxisListType.X

P = 128
D = 128
H, HD = 16, 8
E, F = 14, 256
B, S = 2, 1024
NT = B * S // P
C = 4
NC = NT // C
CB = NC // B
JB = S // P
FC = F // P
MAXP = (B * S - E) // P + E
ROW = D + 2
WB = F + FC
LN_EPS = 1e-5
DENOM_EPS = 1e-6
NOWHERE = 4096
U = 4
GROUPS = [(0, 2)] + [(g, min(g + 4, MAXP)) for g in range(2, MAXP, 4)]
KNOWN = "owners() gives an expert's number, or 0 for a page that nobody has"


def group_of(j):
    return [start <= j < end for start, end in GROUPS].index(True)


def applied_at(j):
    first = [end + (0 if start == 0 else 1) for start, end in GROUPS]
    return [a for a in range(MAXP) if first[group_of(a)] + a - GROUPS[group_of(a)][0] == j]


def build(nc, x, gamma, beta, wqkv, wout, router_w, w1, b1, w2, b2, out):
    with ExitStack() as ctx:
        def sb(name, shape, dt=F32):
            return ctx.enter_context(nc.sbuf_tensor(name, shape, dt))

        def ps(name, shape):
            return ctx.enter_context(nc.psum_tensor(name, shape, F32))

        def sem(name):
            return ctx.enter_context(nc.semaphore(name))

        pages = nc.dram_tensor("pages", [MAXP * P, ROW], F32, kind="Internal").ap()
        out_rows = out.rearrange("b s d -> (b s) d")

        ident = sb("ident", [P, P])
        before = sb("before", [P, P], BF16)
        ones = sb("ones", [P, P], BF16)
        head_mask = sb("head_mask", [P, H])
        prio_i = sb("prio_i", [P, E], I32)
        prio = sb("prio", [P, E])
        eidx_i = sb("eidx_i", [P, E], I32)
        eidx = sb("eidx", [P, E])
        pidx_i = sb("pidx_i", [P, 1], I32)
        pidx = sb("pidx", [P, 1])
        empty_row = sb("empty_row", [P, ROW])
        wqkv_sb = sb("wqkv_sb", [P, 3 * D])
        wout_sb = sb("wout_sb", [P, D])
        rw_sb = sb("rw_sb", [P, E])
        vec_rows = sb("vec_rows", [E * FC + 2, P])
        vec_cols = sb("vec_cols", [P, E * FC + 2])
        w1_sb = sb("w1_sb", [P, E, WB])
        w2_sb = sb("w2_sb", [P, E, FC, D])
        b2_rows = sb("b2_rows", [E, D])
        b2_rest = sb("b2_rest", [E, 2, D])
        b2_part = sb("b2_part", [E, 3, D], BF16)
        b2_k = sb("b2_k", [P, E * D], BF16)

        x_sb = sb("x_sb", [P, NT, D])
        stats = sb("stats", [P, NT, 6])
        mv = sb("mv", [P, NT, 2])
        stats2 = sb("stats2", [P, NT, 6])
        mv2 = sb("mv2", [P, NT, 2])
        ve = sb("ve", [P, NT])
        ve2 = sb("ve2", [P, NT])
        rstd = sb("rstd", [P, NT])
        shift = sb("shift", [P, NT])
        rstd2 = sb("rstd2", [P, NT])
        exponent = sb("exponent", [P, C])
        xn = sb("xn", [P, NT, D])
        xn_t = sb("xn_t", [P, NT, P])
        q_exp = sb("q_exp", [P, NT * P])
        q_pos = sb("q_pos", [P, NT * P])
        q_t = sb("q_t", [P, NT, P])
        k_parts = sb("k_parts", [P, 2 * NT, D])
        k_exp, k_pos = k_parts[:, 0:NT, :], k_parts[:, NT:2 * NT, :]
        k_sb = sb("k_sb", [P, NT, D])
        v_sb = sb("v_sb", [P, NT, D + 1])
        kv_h = sb("kv_h", [P, B, D + H])
        den = sb("den", [P, C, H])
        rden = sb("rden", [P, C, H])
        att = sb("att", [P, NT, D])
        att_t = sb("att_t", [P, NT, P])
        pre = sb("pre", [P, NT, D])
        rows = sb("rows", [P, NT, ROW])
        x1_t = sb("x1_t", [P, NT, P])

        top = sb("top", [P, NT])
        is_top = sb("is_top", [P, C, E])
        ranked = sb("ranked", [P, C, E])
        first = sb("first", [P, NT])
        chosen = sb("chosen", [P, NC, C + 1, E], BF16)
        below = sb("below", [P, NT, E])
        e_exp = sb("e_exp", [P, NT, E])
        e_sum = sb("e_sum", [P, NT])
        cnt = sb("cnt", [P, NC + 1, E])
        cap = sb("cap", [P, NC + 1, E])
        base = sb("base", [P, NC + 1, E])
        used = sb("used", [P, NC + 1])
        cnt_i = sb("cnt_i", [P, E], I32)
        pg_i = sb("pg_i", [P, E], I32)
        LEAD = 8
        pages_had = sb("pages_had", [P, NC + 1, E])
        fresh = sb("fresh", [P, LEAD + E])
        pref = sb("pref", [P, 4, LEAD + E])
        start_pg = sb("start_pg", [P, NC, E])
        end_pg = sb("end_pg", [P, NC, E])
        open_pg = sb("open_pg", [P, E])
        jump = sb("jump", [P, E])
        gets = sb("gets", [P, E])
        room = sb("room", [P, E])
        low = sb("low", [P, E])
        over = sb("over", [P, C, E])
        slot_a = sb("slot_a", [P, C, E])
        slot_b = sb("slot_b", [P, C, E])
        slot_c = sb("slot_c", [P, C, E])
        slot_d = sb("slot_d", [P, C, E])
        slot = sb("slot", [P, NT], I32)
        own_a = sb("own_a", [P, NC, E])
        own_b = sb("own_b", [P, NC, E])
        own_c = sb("own_c", [P, NC, E])
        own_sum = sb("own_sum", [P, 1])
        page_e = sb("page_e", [1, 32], I32)

        xs = sb("xs", [P, U, D])
        xr = sb("xr", [P, MAXP, ROW])
        xs_t = sb("xs_t", [P, U, P])
        w1_cur = sb("w1_cur", [P, U, WB])
        hid = sb("hid", [P, U, FC, P])
        res = k_parts[:, 0:MAXP, :]
        st3 = sb("st3", [P, MAXP, 6])
        mv3 = sb("mv3", [P, MAXP, 2])
        ve3 = sb("ve3", [P, MAXP])
        rstd3 = sb("rstd3", [P, MAXP])
        token = sb("token", [P, MAXP], I32)

        ps_t = ps("ps_t", [P, C, P])
        ps_q = ps("ps_q", [P, C * P])
        ps_kv = ps("ps_kv", [P, C, 2 * D])
        ps_acc = ps("ps_acc", [P, 512])
        ps_num = ps("ps_num", [P, 2, 512])
        ps_o = ps("ps_o", [P, C, P])
        ps_kvh = ps_acc[:, 0:D + 1]
        ps_vec = ps_acc[:, 0:E * FC + 2]
        num_v = ps_num[:, :, 0:2 * (D + H)].rearrange("p b (i n) -> p b i n", i=2)

        def ps_lg(c):
            bank = ps_kv[:, 0, :] if c % 2 else ps_q
            return bank[:, 0:C * E].rearrange("p (i e) -> p i e", e=E)

        def ps_rk(c):
            bank = ps_kv[:, 2, :] if c % 2 else ps_acc
            return bank[:, 0:(C + 1) * E].rearrange("p (i e) -> p i e", e=E)

        ps_row = ps_acc[0:1, 0:32]
        ps_xt = [ps_t[:, 0, :], ps_q[:, 0:P]]
        ps_h = [ps_kv[:, 0, :].rearrange("p (c n) -> p c n", c=FC), ps_kv[:, 2, :].rearrange("p (c n) -> p c n", c=FC)]
        ps_y = [ps_num[:, 0, 0:D], ps_num[:, 1, 0:D]]

        x_in = [sem(f"x_in{c}") for c in range(NC)]
        vec_in, wqkv_in, wout_in, rw_in = sem("vec_in"), sem("wqkv_in"), sem("wout_in"), sem("rw_in")
        w1_in, w2_in, b2_in, b2k_in = sem("w1_in"), sem("w2_in"), sem("b2_in"), sem("b2k_in")
        pages_clear = sem("pages_clear")
        pool_c = sem("pool_c")
        v_ones = sem("v_ones")
        vec_ps, vec_ok, b1_ok = sem("vec_ps"), sem("vec_ok"), sem("b1_ok")
        consts_ok = sem("consts_ok")
        b2_split, b2k_zero = sem("b2_split"), sem("b2k_zero")
        dve_s = sem("dve_s")
        ve_ok, rstd_ok = sem("ve_ok"), sem("rstd_ok")
        ve2_ok, rstd2_ok = sem("ve2_ok"), sem("rstd2_ok")
        ve3_ok, rstd3_ok = sem("ve3_ok"), sem("rstd3_ok")
        shift_ok = sem("shift_ok")
        xn_ok = sem("xn_ok")
        xt_ps, xt_ok = sem("xt_ps"), sem("xt_ok")
        q_ps, kv_ps = sem("q_ps"), sem("kv_ps")
        q_act, k_act, v_ok = sem("q_act"), sem("k_act"), sem("v_ok")
        q_ok, k_ok = sem("q_ok"), sem("k_ok")
        kvh_ps, kvh_ok = sem("kvh_ps"), sem("kvh_ok")
        num_ps, att_ok = sem("num_ps"), sem("att_ok")
        at_ps, at_ok = sem("at_ps"), sem("at_ok")
        wo_ps, pre_ok = sem("wo_ps"), sem("pre_ok")
        x1_ok, x1t_ps, x1t_ok = sem("x1_ok"), sem("x1t_ps"), sem("x1t_ok")
        lg_ps, chosen_ok, below_ok, eexp_ok = sem("lg_ps"), sem("chosen_ok"), sem("below_ok"), sem("eexp_ok")
        weight_ok = sem("weight_ok")
        rk_ps, slot_ok = sem("rk_ps"), sem("slot_ok")
        rows_out = sem("rows_out")
        own_ok, row_ps, page_e_ok = sem("own_ok"), sem("row_ps"), sem("page_e_ok")
        xs_in = [sem(f"xs_in{i}") for i in range(2)]
        xr_in = [sem(f"xr_in{i}") for i in range(2)]
        px_ps, px_ok = sem("px_ps"), sem("px_ok")
        h_ps, hid_ok, y_ps, y_free = sem("h_ps"), sem("hid_ok"), sem("y_ps"), sem("y_free")
        y_ok, st3_ok, mv3_ok = sem("y_ok"), sem("st3_ok"), sem("mv3_ok")
        w1_cur_in = [sem(f"w1_cur_in{k}") for k in range(U)]
        out_in = sem("out_in")

        block = ctx.enter_context(nc.Block())

        N_CONSTS = 11
        (P_IDENT0, P_IDENT, P_BEF0, P_BEFORE, P_ONES, P_HM0, P_HM1, P_HEAD, P_PRIO, P_EIDX, P_PIDX, P_EMPTY0,
         P_EMPTY, P_TOKENS, P_EXPONENT) = range(1, 16)

        def experts(engine):
            return nc.values_load_multi_w_load_instructions(page_e[0:1, 0:MAXP], engines=[engine.engine],
                                                            min_val=0, max_val=E - 1,
                                                            skip_runtime_bounds_check_because=KNOWN)[1]

        @block.sync
        def _(sp):
            def load_x(c):
                b, h = c // CB, c % CB
                src = x[b].rearrange("(p j) d -> p j d", j=JB)[:, C * h:C * h + C, :]
                sp.dma_start(x_sb[:, C * c:C * c + C, :], src).then_inc(x_in[c], 16)

            load_x(0)
            load_x(1)
            load_x(2)
            load_x(3)
            sp.dma_start(wout_sb[:], wout).then_inc(wout_in, 16)
            sp.dma_start(rw_sb[:], router_w).then_inc(rw_in, 16)
            sp.wait_ge(pool_c, P_EMPTY)
            sp.dma_start(pages.rearrange("(j p) d -> p j d", p=P),
                         empty_row[:].unsqueeze(1).to_broadcast([P, MAXP, ROW])).then_inc(pages_clear, 16)
            sp.dma_start(w1_sb[:, :, 0:F], w1.rearrange("e d f -> d e f")).then_inc(w1_in, 16)
            sp.dma_start(w2_sb[:], w2.rearrange("e (c f) d -> f e c d", f=P)).then_inc(w2_in, 16)
            sp.wait_ge(b2_split, 1)
            sp.wait_ge(b2k_zero, 1)
            for i in range(3):
                sp.dma_start(b2_k[i:i + 1, :], b2_part[:, i, :]).then_inc(b2k_in, 16)

            def load_pair(q):
                half = q % 2
                if q >= 2:
                    sp.wait_ge(px_ps, 2 * q - 2)
                    sp.wait_ge(xr_in[half], 16 * (q // 2))
                n = min(2, MAXP - 2 * q)
                src = pages[2 * q * P:(2 * q + n) * P, :].rearrange("(j p) d -> p j d", p=P)
                sp.dma_start(xs[:, 2 * half:2 * half + n, :], src[:, :, 0:D]).then_inc(xs_in[half], 16)
                sp.dma_start(xr[:, 2 * q:2 * q + n, :], src).then_inc(xr_in[half], 16)

            def load_w1(j):
                if j >= U:
                    sp.wait_ge(hid_ok, 2 * (j - U) + 2)
                sp.dma_start(w1_cur[:, j % U, :],
                             w1_sb[:, bass.ds(e[j], 1), :].rearrange("p a n -> p (a n)")).then_inc(w1_cur_in[j % U], 16)

            sp.wait_ge(page_e_ok, 1)
            sp.wait_ge(w1_in, 16)
            sp.wait_ge(b1_ok, 1)
            e = experts(sp)
            for j in range(U):
                load_w1(j)
            sp.wait_ge(rows_out, 16 * NT)
            load_pair(0)
            load_pair(1)
            for q in range(2, (MAXP + 1) // 2):
                load_pair(q)
                for j in (2 * q, 2 * q + 1):
                    if j < MAXP:
                        load_w1(j)
            sp.wait_ge(out_in, 16 * MAXP)

        @block.gpsimd
        def _(pool):
            pool.memset(ident[:], 0.0).then_inc(pool_c, 1)
            pool.wait_ge(pool_c, P_IDENT0)
            pool.affine_select(out=ident[:], in_=ident[:], compare_op=ALU.not_equal, fill=1.0, base=0,
                               pattern=[[-1, P]], channel_multiplier=1).then_inc(pool_c, 1)
            pool.memset(before[:], 1.0).then_inc(pool_c, 1)
            pool.wait_ge(pool_c, P_BEF0)
            pool.affine_select(out=before[:], in_=before[:], compare_op=ALU.is_gt, fill=0.0, base=0,
                               pattern=[[1, P]], channel_multiplier=-1).then_inc(pool_c, 1)
            pool.memset(ones[:], 1.0).then_inc(pool_c, 1)
            pool.memset(head_mask[:], 1.0).then_inc(pool_c, 1)
            pool.wait_ge(pool_c, P_HM0)
            pool.affine_select(out=head_mask[:], in_=head_mask[:], compare_op=ALU.is_ge, fill=0.0, base=0,
                               pattern=[[-HD, H]], channel_multiplier=1).then_inc(pool_c, 1)
            pool.wait_ge(pool_c, P_HM1)
            pool.affine_select(out=head_mask[:], in_=head_mask[:], compare_op=ALU.is_ge, fill=0.0, base=HD - 1,
                               pattern=[[HD, H]], channel_multiplier=-1).then_inc(pool_c, 1)
            pool.iota(prio_i[:], pattern=[[-1, E]], base=E, channel_multiplier=0).then_inc(pool_c, 1)
            pool.iota(eidx_i[:], pattern=[[1, E]], base=0, channel_multiplier=0).then_inc(pool_c, 1)
            pool.iota(pidx_i[:], pattern=[[1, 1]], base=0, channel_multiplier=1).then_inc(pool_c, 1)
            pool.memset(empty_row[:, 0:D + 1], 0.0).then_inc(pool_c, 1)
            pool.iota(empty_row[:, D + 1:ROW].bitcast(I32), pattern=[[1, 1]], base=NOWHERE,
                      channel_multiplier=1).then_inc(pool_c, 1)
            for b in range(B):
                t = pool.iota(rows[:, b * JB:(b + 1) * JB, D + 1].bitcast(I32), pattern=[[1, JB]], base=b * S,
                              channel_multiplier=JB)
            t.then_inc(pool_c, 1)
            pool.memset(v_sb[:, :, D:D + 1], 1.0).then_inc(v_ones, 1)
            pool.memset(exponent[:], -0.5).then_inc(pool_c, 1)

            def power(out_, in_, done):
                pool.tensor_tensor(out_, in_, exponent[:, 0:in_.shape[1]], ALU.pow).then_inc(done, 1)

            def rstd_1(c):
                pool.wait_ge(ve_ok, c + 1)
                power(rstd[:, C * c:C * c + C], ve[:, C * c:C * c + C], rstd_ok)

            def rstd_2(c):
                pool.wait_ge(ve2_ok, c + 1)
                power(rstd2[:, C * c:C * c + C], ve2[:, C * c:C * c + C], rstd2_ok)

            def norm1(c):
                pool.wait_ge(x_in[c], 16)
                pool.wait_ge(shift_ok, c)
                for t in range(C * c, C * c + C):
                    pool.tensor_scalar(xn[:, t, :], x_sb[:, t, :], rstd[:, t:t + 1], shift[:, t:t + 1],
                                       ALU.mult, ALU.add).then_inc(xn_ok, 1)

            pool.wait_ge(pool_c, P_EXPONENT)
            rstd_1(0)
            rstd_1(1)
            norm1(1)
            rstd_1(2)
            norm1(2)
            rstd_1(3)
            norm1(3)
            last_slot = pool.to_reg(MAXP * P - 1)

            def scatter(c):
                pool.wait_ge(x1_ok, c + 1)
                pool.wait_ge(weight_ok, c + 1)
                pool.wait_ge(slot_ok, c + 1)
                for t in range(C * c, C * c + C):
                    pool.indirect_dma_start(pages, bass.IndirectOffsetOnAxis(ap=slot[:, t:t + 1], axis=0),
                                            rows[:, t, :], None, bounds_check=last_slot,
                                            oob_is_err=False).then_inc(rows_out, 16)

            rstd_2(0)
            rstd_2(1)
            pool.wait_ge(pages_clear, 16)
            pool.wait_ge(pool_c, P_TOKENS)
            rstd_2(2)
            rstd_2(3)
            scatter(0)
            scatter(1)
            scatter(2)
            scatter(3)

            last_token = pool.to_reg(B * S - 1)

            pool.wait_ge(page_e_ok, 1)
            stored = 0
            for j in range(MAXP + U + 2):
                for g, (start, end) in enumerate(GROUPS):
                    if end - 1 == j:
                        pool.wait_ge(ve3_ok, g + 1)
                        power(rstd3[:, start:end], ve3[:, start:end], rstd3_ok)
                for a in applied_at(j):
                    stored += 1
                    pool.wait_ge(y_ok, stored)
                    pool.indirect_dma_start(out_rows, bass.IndirectOffsetOnAxis(ap=token[:, a:a + 1], axis=0),
                                            res[:, a, :], None, bounds_check=last_token,
                                            oob_is_err=False).then_inc(out_in, 16)

        @block.scalar
        def _(act):
            act.dma_start(vec_rows[0:E * FC, :], b1.rearrange("e (c f) -> (e c) f", c=FC)).then_inc(vec_in, 16)
            act.dma_start(vec_rows[E * FC:E * FC + 1, :], gamma.rearrange("(a d) -> a d", a=1)).then_inc(vec_in, 16)
            act.dma_start(vec_rows[E * FC + 1:E * FC + 2, :], beta.rearrange("(a d) -> a d", a=1)).then_inc(vec_in, 16)
            act.dma_start(wqkv_sb[:], wqkv).then_inc(wqkv_in, 16)
            act.dma_start(b2_rows[:], b2).then_inc(b2_in, 16)

            def xt(c):
                act.wait_ge(xt_ps, c + 1)
                act.activation(xn_t[:, C * c:C * c + C, :], ps_t[:], ACT.Identity, bias=vec_cols[:, E * FC + 1:E * FC + 2],
                               scale=vec_cols[:, E * FC:E * FC + 1]).then_inc(xt_ok, 1)

            def q(c):
                act.wait_ge(q_ps, c + 1)
                act.activation(q_exp[:, c * C * P:(c + 1) * C * P], ps_q[:], ACT.Exp).then_inc(q_act, 1)
                act.activation(q_pos[:, c * C * P:(c + 1) * C * P], ps_q[:], ACT.Relu).then_inc(q_act, 1)

            def kv(c):
                act.wait_ge(kv_ps, c + 1)
                act.activation(k_exp[:, C * c:C * c + C, :], ps_kv[:, :, 0:D], ACT.Exp).then_inc(k_act, 1)
                act.activation(k_pos[:, C * c:C * c + C, :], ps_kv[:, :, 0:D], ACT.Relu).then_inc(k_act, 1)
                act.copy(v_sb[:, C * c:C * c + C, 0:D], ps_kv[:, :, D:2 * D]).then_inc(v_ok, 1)

            def at(c):
                act.wait_ge(at_ps, c + 1)
                act.copy(att_t[:, C * c:C * c + C, :], ps_o[:]).then_inc(at_ok, 1)

            def x1t(c):
                act.wait_ge(x1t_ps, c + 1)
                act.copy(x1_t[:, C * c:C * c + C, :], ps_t[:]).then_inc(x1t_ok, 1)

            def eexp(c):
                act.wait_ge(below_ok, c + 1)
                act.activation(e_exp[:, C * c:C * c + C, :], below[:, C * c:C * c + C, :], ACT.Exp).then_inc(eexp_ok, 1)

            act.preload_act_table(ACT.Exp)
            act.wait_ge(vec_ok, 1)
            xt(0)
            xt(1)
            q(0)
            kv(0)
            xt(2)
            q(1)
            kv(1)
            xt(3)
            q(2)
            at(0)
            kv(2)
            at(1)
            q(3)
            kv(3)
            x1t(0)
            x1t(1)
            eexp(0)
            at(2)
            eexp(1)
            at(3)
            x1t(2)
            x1t(3)
            eexp(2)
            eexp(3)

            def page_t(j, k):
                act.wait_ge(px_ps, j + 1)
                act.copy(xs_t[:, k, :], ps_xt[k % 2]).then_inc(px_ok, 1)

            def gelu(j, k):
                act.wait_ge(h_ps, j + 1)
                for c in range(FC):
                    act.activation(hid[:, k, c, :], ps_h[k % 2][:, c, :], ACT.Gelu,
                                   bias=w1_cur[:, k, F + c:F + c + 1]).then_inc(hid_ok, 1)

            act.preload_act_table(ACT.Gelu)
            page_t(0, 0)
            page_t(1, 1)
            gelu(0, 0)
            for j in range(MAXP - 1):
                if j + 2 < MAXP:
                    page_t(j + 2, (j + 2) % U)
                gelu(j + 1, (j + 1) % U)

        @block.vector
        def _(dve):
            links = [0]

            def link(ins):
                links[0] += 1
                ins.then_inc(dve_s, 1)
                dve.wait_ge(dve_s, links[0])

            def step(ins):
                links[0] += 1
                ins.then_inc(dve_s, 1)
                return links[0]

            def after(n):
                dve.wait_ge(dve_s, n)

            dve.wait_ge(pool_c, P_PIDX)
            dve.tensor_copy(prio[:], prio_i[:]).then_inc(consts_ok, 1)
            dve.tensor_copy(eidx[:], eidx_i[:]).then_inc(consts_ok, 1)
            dve.tensor_copy(pidx[:], pidx_i[:]).then_inc(consts_ok, 1)
            for z in (cnt, cap, base, pages_had):
                dve.memset(z[:, 0, :], 0.0).then_inc(consts_ok, 1)
            dve.memset(used[:, 0:1], 0.0).then_inc(consts_ok, 1)
            dve.memset(pref[:, :, 0:LEAD], 0.0).then_inc(consts_ok, 1)
            dve.memset(fresh[:, 0:LEAD], 0.0).then_inc(consts_ok, 1)
            dve.memset(chosen[:, :, C, :], 0.0).then_inc(consts_ok, 1)

            def stats1(c):
                dve.wait_ge(x_in[c], 16)
                ts = range(C * c, C * c + C)
                for t in ts:
                    last = dve.bn_stats(stats[:, t, :], x_sb[:, t, :])
                link(last)
                for t in ts:
                    last = dve.bn_aggr(mv[:, t, :], stats[:, t, :])
                link(last)
                dve.tensor_scalar(ve[:, C * c:C * c + C], mv[:, C * c:C * c + C, 1], LN_EPS, None,
                                  ALU.add).then_inc(ve_ok, 1)

            def shift1(c):
                o = slice(C * c, C * c + C)
                dve.wait_ge(rstd_ok, c + 1)
                dve.scalar_tensor_tensor(out=shift[:, o], in0=mv[:, o, 0], scalar=-1.0, in1=rstd[:, o],
                                         op0=ALU.mult, op1=ALU.mult).then_inc(shift_ok, 1)

            stats1(0)
            stats1(1)
            dve.wait_ge(rstd_ok, 1)
            for t in range(C):
                dve.tensor_scalar(xn[:, t, :], x_sb[:, t, :], mv[:, t, 0:1], rstd[:, t:t + 1],
                                  ALU.subtract, ALU.mult).then_inc(xn_ok, 1)
            shift1(1)
            dve.wait_ge(vec_ps, 1)
            dve.tensor_copy(vec_cols[:], ps_vec).then_inc(vec_ok, 1)
            stats1(2)
            dve.wait_ge(b2_in, 16)
            link(dve.tensor_copy(b2_part[:, 0, :], b2_rows[:]))
            link(dve.tensor_tensor(b2_rest[:, 0, :], b2_rows[:], b2_part[:, 0, :], ALU.subtract))
            link(dve.tensor_copy(b2_part[:, 1, :], b2_rest[:, 0, :]))
            link(dve.tensor_tensor(b2_rest[:, 1, :], b2_rest[:, 0, :], b2_part[:, 1, :], ALU.subtract))
            dve.tensor_copy(b2_part[:, 2, :], b2_rest[:, 1, :]).then_inc(b2_split, 1)
            dve.memset(b2_k[:].bitcast(I32), 0).then_inc(b2k_zero, 1)

            def elu_q(c):
                o = slice(c * C * P, (c + 1) * C * P)
                dve.wait_ge(q_act, 2 * c + 2)
                dve.scalar_tensor_tensor(out=q_t[:, C * c:C * c + C, :].rearrange("p i n -> p (i n)"), in0=q_exp[:, o],
                                         scalar=1.0, in1=q_pos[:, o], op0=ALU.min, op1=ALU.add).then_inc(q_ok, 1)

            def elu_k(c):
                o = slice(C * c, C * c + C)
                dve.wait_ge(k_act, 2 * c + 2)
                dve.scalar_tensor_tensor(out=k_sb[:, o, :], in0=k_exp[:, o, :], scalar=1.0, in1=k_pos[:, o, :],
                                         op0=ALU.min, op1=ALU.add).then_inc(k_ok, 1)

            def heads(b):
                dve.wait_ge(kvh_ps, b + 1)
                dve.wait_ge(pool_c, P_HEAD)
                dve.tensor_tensor(kv_h[:, b, 0:D].rearrange("p (h e) -> p h e", e=HD),
                                  ps_kvh[:, 0:D].rearrange("p (h e) -> p h e", e=HD),
                                  head_mask[:].unsqueeze(2).to_broadcast([P, H, HD]), ALU.mult).then_inc(kvh_ok, 1)
                dve.tensor_scalar(kv_h[:, b, D:D + H], head_mask[:], ps_kvh[:, D:D + 1], None,
                                  ALU.mult).then_inc(kvh_ok, 1)

            def divide(c):
                dve.wait_ge(num_ps, c + 1)
                link(dve.tensor_scalar(den[:].rearrange("p (b i) h -> p b i h", b=2), num_v[:, :, :, D:D + H],
                                       DENOM_EPS, None, ALU.add))
                link(dve.reciprocal(rden[:], den[:]))
                for b in range(2):
                    t = C * c + 2 * b
                    dve.tensor_tensor(att[:, t:t + 2, :].rearrange("p i (h e) -> p i h e", e=HD),
                                      num_v[:, b, :, 0:D].rearrange("p i (h e) -> p i h e", e=HD),
                                      rden[:, 2 * b:2 * b + 2, :].unsqueeze(3).to_broadcast([P, 2, H, HD]),
                                      ALU.mult).then_inc(att_ok, 1)

            def stats2_(c):
                ts = range(C * c, C * c + C)
                dve.wait_ge(wo_ps, c + 1)
                dve.scalar_tensor_tensor(out=pre[:, C * c:C * c + C, :], in0=x_sb[:, C * c:C * c + C, :], scalar=2.0,
                                         in1=ps_o[:], op0=ALU.mult, op1=ALU.add).then_inc(pre_ok, 1)
                dve.wait_ge(pre_ok, c + 1)
                for t in ts:
                    last = dve.bn_stats(stats2[:, t, :], pre[:, t, :])
                link(last)
                for t in ts:
                    last = dve.bn_aggr(mv2[:, t, :], stats2[:, t, :])
                link(last)
                dve.tensor_scalar(ve2[:, C * c:C * c + C], mv2[:, C * c:C * c + C, 1], LN_EPS, None,
                                  ALU.add).then_inc(ve2_ok, 1)

            def x1(c):
                dve.wait_ge(rstd2_ok, c + 1)
                for t in range(C * c, C * c + C):
                    last = dve.tensor_scalar(rows[:, t, 0:D], pre[:, t, :], mv2[:, t, 0:1], rstd2[:, t:t + 1],
                                             ALU.subtract, ALU.mult)
                last.then_inc(x1_ok, 1)

            def route(c):
                o = slice(C * c, C * c + C)
                lg = ps_lg(c)
                prio_b = prio[:].unsqueeze(1).to_broadcast([P, C, E])
                top_b = top[:, o].unsqueeze(2).to_broadcast([P, C, E])
                dve.wait_ge(lg_ps, c + 1)
                link(dve.tensor_reduce(top[:, o], lg, AX, ALU.max))
                link(dve.tensor_tensor(is_top[:], lg, top_b, ALU.is_equal))
                link(dve.tensor_tensor(ranked[:], is_top[:], prio_b, ALU.mult))
                link(dve.tensor_reduce(first[:, o], ranked[:], AX, ALU.max))
                dve.tensor_tensor(chosen[:, c, 0:C, :], prio_b, first[:, o].unsqueeze(2).to_broadcast([P, C, E]),
                                  ALU.is_equal).then_inc(chosen_ok, 1)
                dve.tensor_tensor(below[:, o, :], lg, top_b, ALU.subtract).then_inc(below_ok, 1)

            def weigh(c):
                o = slice(C * c, C * c + C)
                dve.wait_ge(eexp_ok, c + 1)
                link(dve.tensor_reduce(e_sum[:, o], e_exp[:, o, :], AX, ALU.add))
                dve.reciprocal(rows[:, o, D], e_sum[:, o]).then_inc(weight_ok, 1)

            def place(c):
                rk = ps_rk(c)

                def each(a):
                    return a.unsqueeze(1).to_broadcast([P, C, E])

                dve.tensor_tensor(room[:], cap[:, c, :], cnt[:, c, :], ALU.subtract)
                dve.tensor_tensor(low[:], base[:, c, :], cnt[:, c, :], ALU.add)
                ahead = step(dve.tensor_tensor(open_pg[:], base[:, c, :], cap[:, c, :], ALU.add))
                dve.wait_ge(rk_ps, c + 1)
                a = step(dve.scalar_tensor_tensor(out=cnt_i[:], in0=rk[:, C, :], scalar=float(P - 1),
                                                  in1=cnt[:, c, :], op0=ALU.add, op1=ALU.add))
                dve.tensor_tensor(cnt[:, c + 1, :], cnt[:, c, :], rk[:, C, :], ALU.add)
                after(a)
                a = step(dve.tensor_scalar(pg_i[:], cnt_i[:], 7, None, ALU.logical_shift_right))
                over_ = step(dve.tensor_tensor(over[:], rk[:, 0:C, :], each(room[:]), ALU.is_ge))
                after(a)
                a = step(dve.tensor_tensor(fresh[:, LEAD:], pg_i[:], pages_had[:, c, :], ALU.subtract))
                dve.tensor_copy(pages_had[:, c + 1, :], pg_i[:])
                after(a)
                src, b = fresh, None
                for s, d in enumerate((1, 2, 4, 8)):
                    a = step(dve.tensor_tensor(pref[:, s, LEAD:], src[:, LEAD:], src[:, LEAD - d:LEAD - d + E], ALU.add))
                    if s == 0:
                        b = step(dve.tensor_tensor(slot_b[:], rk[:, 0:C, :], each(low[:]), ALU.add))
                    if s == 1:
                        dve.tensor_scalar(cap[:, c + 1, :], pg_i[:], float(P), None, ALU.mult)
                    after(a)
                    src = pref[:, s]
                link(dve.scalar_tensor_tensor(out=start_pg[:, c, :], in0=src[:, LEAD:], scalar=used[:, c:c + 1],
                                              in1=fresh[:, LEAD:], op0=ALU.add, op1=ALU.subtract))
                a = step(dve.scalar_tensor_tensor(out=jump[:], in0=start_pg[:, c, :], scalar=float(P), in1=open_pg[:],
                                                  op0=ALU.mult, op1=ALU.subtract))
                dve.tensor_scalar(used[:, c + 1:c + 2], src[:, LEAD + E - 1:LEAD + E], used[:, c:c + 1], None, ALU.add)
                after(a)
                a = step(dve.tensor_tensor(slot_a[:], over[:], each(jump[:]), ALU.mult))
                g = step(dve.scalar_tensor_tensor(out=gets[:], in0=fresh[:, LEAD:], scalar=0.0, in1=jump[:],
                                                  op0=ALU.is_gt, op1=ALU.mult))
                after(a)
                a = step(dve.tensor_tensor(slot_c[:], slot_a[:], slot_b[:], ALU.add))
                after(g)
                dve.tensor_tensor(base[:, c + 1, :], base[:, c, :], gets[:], ALU.add)
                after(a)
                a = step(dve.tensor_tensor(slot_d[:], slot_c[:], chosen[:, c, 0:C, :], ALU.mult))
                step(dve.tensor_tensor(end_pg[:, c, :], start_pg[:, c, :], fresh[:, LEAD:], ALU.add))
                after(a)
                with nc.allow_low_precision(reason="slots are whole numbers below 2**24"):
                    dve.tensor_reduce(slot[:, C * c:C * c + C], slot_d[:], AX, ALU.add).then_inc(slot_ok, 1)

            def owners():
                link(dve.tensor_scalar(own_a[:], start_pg[:], pidx[:, 0:1], None, ALU.is_le))
                link(dve.tensor_scalar(own_b[:], end_pg[:], pidx[:, 0:1], None, ALU.is_gt))
                link(dve.tensor_tensor(own_c[:], own_a[:], own_b[:], ALU.mult))
                link(dve.tensor_tensor(own_a[:], own_c[:], eidx[:].unsqueeze(1).to_broadcast([P, NC, E]), ALU.mult))
                dve.tensor_reduce(own_sum[:], own_a[:].rearrange("p c e -> p (c e)"), AX, ALU.add).then_inc(own_ok, 1)

            shift1(2)
            stats1(3)
            elu_q(0)
            shift1(3)
            elu_k(0)
            elu_q(1)
            elu_k(1)
            dve.wait_ge(consts_ok, N_CONSTS)
            heads(0)
            divide(0)
            elu_q(2)
            divide(1)
            stats2_(0)
            elu_k(2)
            elu_q(3)
            x1(0)
            stats2_(1)
            elu_k(3)
            x1(1)
            route(0)
            heads(1)
            weigh(0)
            divide(2)
            route(1)
            divide(3)
            stats2_(2)
            place(0)
            stats2_(3)
            x1(2)
            weigh(1)
            x1(3)
            place(1)
            route(2)
            weigh(2)
            place(2)
            route(3)
            place(3)
            weigh(3)
            owners()
            dve.wait_ge(row_ps, 1)
            dve.tensor_copy(page_e[:], ps_row[:, 0:32]).then_inc(page_e_ok, 1)
            dve.wait_ge(w1_in, 16)
            dve.tensor_copy(w1_sb[:, :, F:WB],
                            vec_cols[:, 0:E * FC].rearrange("p (e c) -> p e c", c=FC)).then_inc(b1_ok, 1)

            def residual(j):
                dve.wait_ge(xr_in[j // 2 % 2], 16 * (j // 4) + 16)
                dve.wait_ge(y_ps, j + 1)
                dve.scalar_tensor_tensor(out=res[:, j, :], in0=ps_y[j % 2], scalar=xr[:, j, D:D + 1],
                                         in1=xr[:, j, 0:D], op0=ALU.mult, op1=ALU.add).then_inc(y_free, 1)

            def apply(j):
                dve.wait_ge(rstd3_ok, group_of(j) + 1)
                dve.tensor_scalar(res[:, j, :], res[:, j, :], mv3[:, j, 0:1], rstd3[:, j:j + 1],
                                  ALU.subtract, ALU.mult).then_inc(y_ok, 1)

            for j in range(MAXP + U + 2):
                if j < MAXP:
                    residual(j)
                    dve.wait_ge(y_free, j + 1)
                    dve.bn_stats(st3[:, j, :], res[:, j, :]).then_inc(st3_ok, 1)
                for a in applied_at(j):
                    apply(a)
                if j < MAXP:
                    dve.wait_ge(st3_ok, j + 1)
                    dve.bn_aggr(mv3[:, j, :], st3[:, j, :]).then_inc(mv3_ok, 1)
                for start, end in GROUPS:
                    if end - 1 == j:
                        dve.tensor_copy(token[:, start:end], xr[:, start:end, D + 1].bitcast(I32))
                        dve.wait_ge(mv3_ok, end)
                        dve.tensor_scalar(ve3[:, start:end], mv3[:, start:end, 1], LN_EPS, None,
                                          ALU.add).then_inc(ve3_ok, 1)

        @block.tensor
        def _(pe):
            def mm(o, l, r, start=True, stop=True):
                return pe.matmul(o, l, r, start=start, stop=stop)

            def tr_x(c):
                pe.wait_ge(xn_ok, C * c + C)
                if c:
                    pe.wait_ge(xt_ok, c)
                for i in range(C):
                    last = pe.transpose(ps_t[:, i, :], xn[:, C * c + i, :], ident[:])
                last.then_inc(xt_ps, 1)

            def proj_q(c):
                pe.wait_ge(xt_ok, c + 1)
                if c:
                    pe.wait_ge(q_act, 2 * c)
                mm(ps_q[:], wqkv_sb[:, 0:D], xn_t[:, C * c:C * c + C, :].rearrange("p i n -> p (i n)")).then_inc(q_ps, 1)

            def proj_kv(c):
                if c:
                    pe.wait_ge(v_ok, c)
                    pe.wait_ge(k_act, 2 * c)
                for i in range(C):
                    last = mm(ps_kv[:, i, :], xn_t[:, C * c + i, :], wqkv_sb[:, D:3 * D])
                last.then_inc(kv_ps, 1)

            def sum_kv(c):
                if c == CB:
                    pe.wait_ge(kvh_ok, 2)
                pe.wait_ge(k_ok, c + 1)
                pe.wait_ge(v_ok, c + 1)
                for t in range(C * c, C * c + C):
                    last = mm(ps_kvh, k_sb[:, t, :], v_sb[:, t, :], t % JB == 0, t % JB == JB - 1)
                if c % CB == CB - 1:
                    last.then_inc(kvh_ps, 1)

            def num(c):
                pe.wait_ge(kvh_ok, 2 * (c // CB) + 2)
                pe.wait_ge(q_ok, c + 1)
                if c:
                    pe.wait_ge(att_ok, 2 * c)
                for i in range(C):
                    last = mm(num_v[:, i // 2, i % 2, :], q_t[:, C * c + i, :], kv_h[:, c // CB, :])
                last.then_inc(num_ps, 1)

            def tr_att(c):
                pe.wait_ge(att_ok, 2 * c + 2)
                if c:
                    pe.wait_ge(pre_ok, c)
                for i in range(C):
                    last = pe.transpose(ps_o[:, i, :], att[:, C * c + i, :], ident[:])
                last.then_inc(at_ps, 1)

            def proj_out(c):
                pe.wait_ge(at_ok, c + 1)
                for i in range(C):
                    last = mm(ps_o[:, i, :], att_t[:, C * c + i, :], wout_sb[:])
                last.then_inc(wo_ps, 1)

            def tr_x1(c):
                pe.wait_ge(x1_ok, c + 1)
                pe.wait_ge(xt_ok, NC)
                if c:
                    pe.wait_ge(x1t_ok, c)
                for i in range(C):
                    last = pe.transpose(ps_t[:, i, :], rows[:, C * c + i, 0:D], ident[:])
                last.then_inc(x1t_ps, 1)

            def logits(c):
                pe.wait_ge(x1t_ok, c + 1)
                if c == 0:
                    pe.wait_ge(q_act, 2 * NC)
                elif c == 1:
                    pe.wait_ge(k_act, 2 * NC)
                    pe.wait_ge(v_ok, NC)
                else:
                    pe.wait_ge(below_ok, c - 1)
                for i in range(C):
                    last = mm(ps_lg(c)[:, i, :], x1_t[:, C * c + i, :], rw_sb[:])
                last.then_inc(lg_ps, 1)

            def ranks(c):
                pe.wait_ge(chosen_ok, c + 1)
                if c == 0:
                    pe.wait_ge(kvh_ok, 2 * B)
                elif c >= 2:
                    pe.wait_ge(slot_ok, c - 1)
                rk = ps_rk(c)
                mm(rk, before[:], chosen[:, c, :, :], True, False)
                for i in range(C):
                    last = mm(rk[:, i + 1:C + 1, :], ones[:],
                              chosen[:, c, i:i + 1, :].to_broadcast([P, C - i, E]), False, i == C - 1)
                last.then_inc(rk_ps, 1)

            pe.wait_ge(pool_c, P_IDENT)
            pe.wait_ge(vec_in, 48)
            pe.transpose(ps_vec, vec_rows[:], ident[0:E * FC + 2, 0:E * FC + 2]).then_inc(vec_ps, 1)
            tr_x(0)
            tr_x(1)
            pe.wait_ge(wqkv_in, 16)
            proj_q(0)
            proj_kv(0)
            tr_x(2)
            proj_q(1)
            proj_kv(1)
            pe.wait_ge(v_ones, 1)
            pe.wait_ge(vec_ok, 1)
            sum_kv(0)
            tr_x(3)
            proj_q(2)
            sum_kv(1)
            num(0)
            proj_kv(2)
            tr_att(0)
            num(1)
            pe.wait_ge(wout_in, 16)
            proj_out(0)
            proj_q(3)
            tr_att(1)
            proj_kv(3)
            proj_out(1)
            sum_kv(2)
            tr_x1(0)
            pe.wait_ge(rw_in, 16)
            logits(0)
            tr_x1(1)
            sum_kv(3)
            num(2)
            pe.wait_ge(pool_c, P_ONES)
            pe.wait_ge(consts_ok, N_CONSTS)
            ranks(0)
            logits(1)
            tr_att(2)
            num(3)
            proj_out(2)
            ranks(1)
            tr_att(3)
            proj_out(3)
            tr_x1(2)
            logits(2)
            tr_x1(3)
            ranks(2)
            logits(3)
            ranks(3)
            pe.wait_ge(own_ok, 1)
            mm(ps_row, own_sum[:], ident[:, 0:32]).then_inc(row_ps, 1)

            def turn(j):
                pe.wait_ge(xs_in[j // 2 % 2], 16 * (j // 4) + 16)
                pe.transpose(ps_xt[j % 2], xs[:, j % U, :], ident[:]).then_inc(px_ps, 1)

            def hidden(j):
                pe.wait_ge(px_ok, j + 1)
                pe.wait_ge(w1_cur_in[j % U], 16 * (j // U) + 16)
                for c in range(FC):
                    last = mm(ps_h[j % 2][:, c, :], w1_cur[:, j % U, c * P:(c + 1) * P], xs_t[:, j % U, :])
                last.then_inc(h_ps, 1)

            def output(j):
                pe.wait_ge(hid_ok, 2 * j + 2)
                if j >= 2:
                    pe.wait_ge(y_free, j - 1)
                for c in range(FC):
                    mm(ps_y[j % 2], hid[:, j % U, c, :], w2_sb[:, bass.ds(e[j], 1), c, :].rearrange("p a n -> p (a n)"),
                       c == 0, False)
                mm(ps_y[j % 2], ones[:], b2_k[:, bass.ds(e[j] * D, D)], False, True).then_inc(y_ps, 1)

            pe.wait_ge(page_e_ok, 1)
            e = experts(pe)
            pe.wait_ge(w2_in, 16)
            pe.wait_ge(b2k_in, 48)
            pe.wait_ge(x1t_ok, NC)
            turn(0)
            turn(1)
            hidden(0)
            for j in range(MAXP):
                if j + 2 < MAXP:
                    turn(j + 2)
                if j + 1 < MAXP:
                    hidden(j + 1)
                output(j)


INPUTS = ["L0_attn_x", "L0_attn_gamma", "L0_attn_beta", "L0_attn_Wqkv", "L0_attn_Wout", "L0_ffn_router_w",
          "L0_ffn_w1", "L0_ffn_b1", "L0_ffn_w2", "L0_ffn_b2"]


def kernel(**inputs):
    import numpy as np
    import concourse.bacc as bacc
    from concourse.bass_utils import run_bass_kernel_spmd

    nc = bacc.Bacc("TRN2", target_bir_lowering=False, num_devices=1)
    arrays, args = {}, []
    for name in INPUTS:
        arrays[name] = np.ascontiguousarray(inputs[name])
        args.append(nc.dram_tensor(name, arrays[name].shape, F32, kind="ExternalInput").ap())
    out = nc.dram_tensor("out", arrays["L0_attn_x"].shape, F32, kind="ExternalOutput").ap()
    build(nc, *args, out)
    result = run_bass_kernel_spmd(nc, [arrays], core_ids=[0])
    return result.results[0]["out"]
```
